# Optimizing a Trainium2 kernel written in Bass

```python
import numpy as np
import jax
import jax.numpy as jnp

def _softmax(x, axis=-1):
    return jax.nn.softmax(x, axis=axis)

def _gelu(x):
    return jax.nn.gelu(x, approximate=True)

def _silu(x):
    return jax.nn.silu(x)

def _sigmoid(x):
    return jax.nn.sigmoid(x)

def _layernorm(x, axis=-1, eps=1e-05):
    m = jnp.mean(x, axis=axis, keepdims=True)
    v = jnp.var(x, axis=axis, keepdims=True)
    return (x - m) / jnp.sqrt(v + eps)

def _scatter_add(tgt, idx, src, axis=0):
    return tgt.at[idx].add(src)

def _segment_sum(src, seg, n):
    return jax.ops.segment_sum(src, seg, n)
kernel_name = 'mk_flamingo_gated_d1_seqx_r8_10fcb5'

def setup_inputs(seed: int=0):
    np.random.seed(seed)
    _w = jnp.asarray

    def _rec_inputs():
        import jax
        import jax.numpy as jnp
        _rk = jax.random.key(seed)
        x = -0.0002928 + 1 * jax.random.normal(jax.random.fold_in(_rk, 1), (16, 128, 128), jnp.float32)
        _lenS = 128 - jax.random.randint(jax.random.fold_in(_rk, 7), (16,), 0, max(1, 128 // 4) + 1, jnp.int32)
        _lenS2 = 128 - jax.random.randint(jax.random.fold_in(_rk, 8), (16,), 0, max(1, 128 // 4) + 1, jnp.int32)
        _ctx_1024P = jax.random.normal(jax.random.fold_in(_rk, 11), (16, 16, 128), jnp.float32)
        _ctx_1024c = jax.random.dirichlet(jax.random.fold_in(_rk, 511), 0.3 * jnp.ones((16,), jnp.float32), (16, 128))
        _ctx_1024t = jnp.einsum('bsk,bkd->bsd', _ctx_1024c, _ctx_1024P)
        _ctx_1024t = _ctx_1024t * jax.lax.rsqrt(jnp.mean(jnp.square(_ctx_1024t)) + 1e-12) * 0.953939
        ctx_1024 = -1.39393e-06 + 0.999914 * (_ctx_1024t + 0.3 * jax.random.normal(jax.random.fold_in(_rk, 611), (16, 128, 128), jnp.float32))
        _g = jax.random.normal(jax.random.fold_in(_rk, 9001), (2, 1), jnp.float32)
        _g = jnp.sign(_g) * jnp.maximum(jnp.abs(_g), 1.0) + (_g == 0) * 1.0
        g_xattn = _g[0]
        g_ffn = _g[1]
        return (x, ctx_1024, g_xattn, g_ffn)
    x, ctx_1024, g_xattn, g_ffn = _rec_inputs()

    def _L0_xattn_setup():
        import jax, jax.numpy as jnp
        import numpy as np
        B, T, D, H = (2, 256, 128, 16)
        DH = D // H
        key = jax.random.key(seed)
        ks = jax.random.split(key, 11)
        s = 1.0 / np.sqrt(D)
        return {'q': jax.random.normal(ks[0], (B, T, D), jnp.float32), 'k': jax.random.normal(ks[1], (B, T, D), jnp.float32), 'v': jax.random.normal(ks[2], (B, T, D), jnp.float32), 'wq_w': jax.random.normal(ks[3], (D, D), jnp.float32) * s, 'wq_b': jnp.zeros((D,), jnp.float32), 'wk_w': jax.random.normal(ks[4], (D, D), jnp.float32) * s, 'wk_b': jnp.zeros((D,), jnp.float32), 'wv_w': jax.random.normal(ks[5], (D, D), jnp.float32) * s, 'wv_b': jnp.zeros((D,), jnp.float32), 'wo_w': jax.random.normal(ks[6], (D, D), jnp.float32) * s, 'wo_b': jnp.zeros((D,), jnp.float32)}
    _L0_xattn_all = _L0_xattn_setup()
    _L0_xattn_in = {k: v for k, v in _L0_xattn_all.items() if k in ('wq_w', 'wq_b', 'wk_w', 'wk_b', 'wv_w', 'wv_b', 'wo_w', 'wo_b')}
    del _L0_xattn_all

    def _L0_ffn_setup():
        import jax, jax.numpy as jnp
        import numpy as np
        B, S, D, H, E = (4, 256, 128, 512, 8)
        key = jax.random.key(seed)
        ks = jax.random.split(key, 8)
        s_d = 1.0 / np.sqrt(D)
        s_h = 1.0 / np.sqrt(H)
        return {'x': jax.random.normal(ks[0], (B, S, D), dtype=jnp.float32), 'gate_w': jax.random.uniform(ks[1], (E, D), jnp.float32, -s_d, s_d), 'gate_b': jax.random.uniform(ks[2], (E,), jnp.float32, -s_d, s_d), 'w1': jax.random.uniform(ks[3], (E, H, D), jnp.float32, -s_d, s_d), 'b1': jax.random.uniform(ks[4], (E, H), jnp.float32, -s_d, s_d), 'w2': jax.random.uniform(ks[5], (E, D, H), jnp.float32, -s_h, s_h), 'b2': jax.random.uniform(ks[6], (E, D), jnp.float32, -s_h, s_h)}
    _L0_ffn_all = _L0_ffn_setup()
    _L0_ffn_in = {k: v for k, v in _L0_ffn_all.items() if k in ('gate_w', 'gate_b', 'w1', 'b1', 'w2', 'b2')}
    del _L0_ffn_all
    return {'x': x, 'ctx_1024': ctx_1024, 'g_xattn': g_xattn, 'g_ffn': g_ffn, 'L0_xattn_wq_w': _L0_xattn_in['wq_w'], 'L0_xattn_wq_b': _L0_xattn_in['wq_b'], 'L0_xattn_wk_w': _L0_xattn_in['wk_w'], 'L0_xattn_wk_b': _L0_xattn_in['wk_b'], 'L0_xattn_wv_w': _L0_xattn_in['wv_w'], 'L0_xattn_wv_b': _L0_xattn_in['wv_b'], 'L0_xattn_wo_w': _L0_xattn_in['wo_w'], 'L0_xattn_wo_b': _L0_xattn_in['wo_b'], 'L0_ffn_gate_w': _L0_ffn_in['gate_w'], 'L0_ffn_gate_b': _L0_ffn_in['gate_b'], 'L0_ffn_w1': _L0_ffn_in['w1'], 'L0_ffn_b1': _L0_ffn_in['b1'], 'L0_ffn_w2': _L0_ffn_in['w2'], 'L0_ffn_b2': _L0_ffn_in['b2']}

def reference(x, ctx_1024, g_xattn, g_ffn, L0_xattn_wq_w, L0_xattn_wq_b, L0_xattn_wk_w, L0_xattn_wk_b, L0_xattn_wv_w, L0_xattn_wv_b, L0_xattn_wo_w, L0_xattn_wo_b, L0_ffn_gate_w, L0_ffn_gate_b, L0_ffn_w1, L0_ffn_b1, L0_ffn_w2, L0_ffn_b2):
    import jax
    import jax.numpy as jnp

    def _L0_xattn_ref(q, k, v, wq_w, wq_b, wk_w, wk_b, wv_w, wv_b, wo_w, wo_b):
        import jax, jax.numpy as jnp
        import numpy as np
        B, T, D, H = (2, 256, 128, 16)
        DH = D // H
        b, t, d = q.shape
        wq = (q @ wq_w.T + wq_b).reshape(b, t, H, DH)
        wk = (k @ wk_w.T + wk_b).reshape(b, t, H, DH)
        wv = (v @ wv_w.T + wv_b).reshape(b, t, H, DH)
        scores = jnp.einsum('bthd,bshd->bhts', wq, wk) / jnp.sqrt(jnp.float32(DH))
        probs = jax.nn.softmax(scores, axis=-1)
        attn = jnp.einsum('bhts,bshd->bthd', probs, wv)
        attn = attn.reshape(b, t, d)
        return attn @ wo_w.T + wo_b

    def _L0_ffn_ref(x, gate_w, gate_b, w1, b1, w2, b2):
        import jax, jax.numpy as jnp
        import numpy as np
        B, S, D, H, E = (4, 256, 128, 512, 8)
        b, s, d = x.shape
        xf = x.reshape(-1, d)
        logits = xf @ gate_w.T + gate_b
        top1 = jnp.argmax(logits, axis=-1)
        out = jnp.zeros_like(xf)
        n_experts = w1.shape[0]
        for e in range(n_experts):
            h = jax.nn.relu(xf @ w1[e].T + b1[e])
            y = h @ w2[e].T + b2[e]
            out = out + jnp.where((top1 == e)[:, None], y, jnp.zeros((), y.dtype))
        return out.reshape(b, s, d)
    x = x + jnp.tanh(g_xattn[0]) * _L0_xattn_ref(_layernorm(x, axis=-1), ctx_1024, ctx_1024, L0_xattn_wq_w, L0_xattn_wq_b, L0_xattn_wk_w, L0_xattn_wk_b, L0_xattn_wv_w, L0_xattn_wv_b, L0_xattn_wo_w, L0_xattn_wo_b)
    x = x + jnp.tanh(g_ffn[0]) * _L0_ffn_ref(_layernorm(x, axis=-1), L0_ffn_gate_w, L0_ffn_gate_b, L0_ffn_w1, L0_ffn_b1, L0_ffn_w2, L0_ffn_b2)
    return x

_drawn_inputs = setup_inputs


def setup_inputs(seed=0):
    import zlib

    import numpy as np

    out = dict(_drawn_inputs(seed))
    spreads = {'L0_xattn_wq_b': (0.0, 0.1),
     'L0_xattn_wk_b': (0.0, 0.8),
     'L0_xattn_wv_b': (0.0, 0.1),
     'L0_xattn_wo_b': (0.0, 0.1)}
    factors = {'L0_ffn_b1': 3.234}
    for name, (base, spread) in spreads.items():
        noise = np.random.default_rng([zlib.crc32(name.encode()), seed]).standard_normal(out[name].shape)
        drawn = base * np.exp(spread * noise) if base else spread * noise
        out[name] = jnp.asarray(drawn.astype(out[name].dtype))
    for name, factor in factors.items():
        out[name] = (out[name] * factor).astype(out[name].dtype)
    return out
```

```python
import concourse.bass as bass
from concourse import mybir
from contextlib import ExitStack

F32 = mybir.dt.float32
F16 = mybir.dt.float16
BF16 = mybir.dt.bfloat16
I32 = mybir.dt.int32
U32 = mybir.dt.uint32
ALU = mybir.AluOpType
ACT = mybir.ActivationFunctionType
AX = mybir.AxisListType

NB, T, D = 16, 128, 128
NTOK = NB * T
NH, DH = 16, 8
NG = 4
SLOT = 32
NE, HID = 8, 512
HC = HID // 128
NBLK = NTOK // 128 + NE - 1
CB = 4
NC = NB // CB
CT = CB * T
EPS = 1e-5
SCALE = float(DH) ** -0.5
VC = 2 * (DH + 1)
ROW = 2 * D + 8
W_W2, W_B1, W_B2 = HID, HID + HC * D, HID + HC * D + HC
WCOL = W_B2 + D

C_ID, C_J, C_E, C_B = 0, 128, 128 + NE * NB, 128 + NE * NB + NE
C_TOK = C_B + NBLK * NE
NCONST = C_TOK + NB


def program(nc, x, ctxT, wqkvoT, gateT, cols, rows, gate_b, gains, wexp, b2r, constf, consth, onesh, out):
    ctx = ExitStack()
    with ctx:
        def sb(name, shape, dt=F32):
            return ctx.enter_context(nc.sbuf_tensor(name, shape, dt))

        def ps(name, shape, dt=F32):
            return ctx.enter_context(nc.psum_tensor(name, shape, dt))

        def sem(name):
            return ctx.enter_context(nc.semaphore(name))

        q_dram = nc.dram_tensor("q_stack", (NG, 4, 3, DH, NTOK), F16).ap()
        k_dram = nc.dram_tensor("k_stack", (NG, 4, 4, DH, NTOK), F16).ap()
        m_dram = nc.dram_tensor("neg_max", (NB, 4, 2, NG, T), F16).ap()
        sorted_dram = nc.dram_tensor("sorted_rows", (NBLK * 128, ROW), F32).ap()

        x_sb = sb("x_sb", [128, NB, D])
        ctx_sb = sb("ctx_sb", [128, NTOK])
        w_sb = sb("w_sb", [128, 4, D])
        gate_sb = sb("gate_sb", [128, NE])
        cols_sb = sb("cols_sb", [128, 2])
        rows_sb = sb("rows_sb", [128, 2, D])
        gateb_sb = sb("gateb_sb", [128, NE])
        gains_sb = sb("gains_sb", [128, 2])
        tg = sb("tg", [128, 2])
        cf = sb("cf", [128, NCONST])
        ch = sb("ch", [128, 3 * 128], F16)
        experts = sb("experts", [128, NE, WCOL])
        ident = cf[:, C_ID:C_ID + 128]
        ident_h = ch[:, 0:128]
        before_h = ch[:, 128:256]
        ones_h = ch[:, 256:384]

        stats = sb("stats", [128, NB, 6])
        mv = sb("mv", [128, NB, 2])
        ve1 = sb("ve1", [128, NB])
        std = sb("std", [128, NB])
        rstd = sb("rstd", [128, NB])
        nmr = sb("nmr", [128, NB])
        q_part = sb("q_part", [128, 2, 2, CT], F16)
        k_part = sb("k_part", [128, 2, 2, CT], F16)
        v_sb = sb("v_sb", [128, NB, NH, VC], F16)
        q_st = sb("q_st", [128, NG, 4, NTOK], F16)
        k_st = sb("k_st", [128, NG, NTOK], F16)
        gbo = sb("gbo", [128, D])

        mx = sb("mx", [128, 2, NH])
        mcol = sb("mcol", [128, 2, 32], F16)
        mT = sb("mT", [32, 2, T], F16)
        prob = sb("prob", [128, 2, NH * T])
        xn = prob[:, 0, 0:2 * CT].rearrange("p (n b d) -> p n b d", n=2, b=CB)
        xnT = prob[:, 0, 2 * CT:4 * CT].rearrange("p (n t) -> p n t", n=2)
        v32 = prob[:, 1, 0:2 * CT].rearrange("p (n b d) -> p n b d", n=2, b=CB)
        prob_lo = sb("prob_lo", [128, 2, NH * T], F16)
        usum = sb("usum", [128, NH, DH + 1])
        rden = sb("rden", [128, NH])
        attn = sb("attn", [128, 2, D])
        attnT = sb("attnT", [128, 2, T])
        token_row = sb("token_row", [128, NB, ROW])
        stats2 = sb("stats2", [128, NB, 6])
        mv2 = sb("mv2", [128, NB, 2])
        ve2 = sb("ve2", [128, NB])
        mhalf = sb("mhalf", [128, NB])
        rstd2 = sb("rstd2", [128, NB])
        nmr2 = sb("nmr2", [128, NB])
        x2T = sb("x2T", [128, 2, T])
        logit = sb("logit", [128, NB, NE])

        lmax = sb("lmax", [128, NB])
        isbest = sb("isbest", [128, NB, NE])
        picked = sb("picked", [128, NB, NE])
        wgt = sb("wgt", [128, NB, NE])
        onehot_h = sb("onehot_h", [128, NB, NE], F16)
        base = sb("base", [128, NB, NE])
        wmax = sb("wmax", [128, NB])
        ones8 = sb("ones8", [128, NE])
        nbc = sb("nbc", [128, NE, NB])
        nblk = sb("nblk", [128, NE])
        bend = sb("bend", [128, NE])
        bstart = sb("bstart", [128, NE])
        slotf = sb("slotf", [128, NB])
        slot = sb("slot", [128, NB], U32)
        ble = sb("ble", [128, NBLK, NE])
        bexpf = sb("bexpf", [128, NBLK])
        bexp = sb("bexp", [128, NBLK + 1], I32)

        fill = sb("fill", [128, ROW])
        q_words = q_st[:].rearrange("p g i t -> p (g i t)").bitcast(F32)
        taken = [0]

        def over_q(*shape):
            size = 1
            for n in shape:
                size *= n
            at, taken[0] = taken[0], taken[0] + size
            names = "abc"[:len(shape)]
            return q_words[:, at:at + size].rearrange(f"p ({' '.join(names)}) -> p {' '.join(names)}",
                                                      **dict(zip(names, shape)))

        blk = over_q(3, ROW)
        wblk = over_q(2, WCOL)
        bT = over_q(2, 128)
        hT = over_q(2, HC, 128)
        res = over_q(2, D)
        outb = over_q(2, D)

        bankA = ps("bankA", [128, 512])
        bankC = ps("bankC", [128, 4 * 512])
        bankU = ps("bankU", [128, 512])
        bankT = ps("bankT", [128, 512])
        bankM = ps("bankM", [128, 512])
        bankC_ = [bankC[:, 512 * i:512 * i + 512] for i in range(4)]

        ld_const = sem("ld_const")
        ld_w = sem("ld_w")
        ld_small = sem("ld_small")
        ld_exp = sem("ld_exp")
        ld_b2 = sem("ld_b2")
        ld_x = [sem(f"ld_x{c}") for c in range(NC)]
        ld_ctx = [sem(f"ld_ctx{c}") for c in range(NC)]
        q_zero = [sem(f"q_zero{c}") for c in range(NC)]
        v_init = sem("v_init")
        ids_done = sem("ids_done")
        fill_done = sem("fill_done")
        sorted_init = sem("sorted_init")
        ones_in_k = sem("ones_in_k")
        bn1 = sem("bn1")
        agg1 = sem("agg1")
        eps1 = sem("eps1")
        std1 = sem("std1")
        rst1 = sem("rst1")
        nmr1 = sem("nmr1")
        xn_done = sem("xn_done")
        xnT_mm = sem("xnT_mm")
        xnT_ev = sem("xnT_ev")
        q_mm = sem("q_mm")
        k_mm = sem("k_mm")
        v_mm = sem("v_mm")
        q_hi = sem("q_hi")
        q_lo = sem("q_lo")
        k_hi = sem("k_hi")
        k_lo = sem("k_lo")
        v_32 = sem("v_32")
        v_hi = sem("v_hi")
        v_lo = sem("v_lo")
        q_written = [sem(f"q_written{c}") for c in range(NC)]
        k_written = [sem(f"k_written{c}") for c in range(NC)]
        q_ready = [sem(f"q_ready{c}") for c in range(NC)]
        k_ready = [sem(f"k_ready{c}") for c in range(NC)]
        tg_done = sem("tg_done")
        gbo_done = sem("gbo_done")
        xb_done = sem("xb_done")
        b2g_done = sem("b2g_done")

        s1_mm = sem("s1_mm")
        max_done = sem("max_done")
        m_hi = sem("m_hi")
        m_lo = sem("m_lo")
        mT_mm = sem("mT_mm")
        mT_ev = sem("mT_ev")
        m_written = sem("m_written")
        m_ready = [sem(f"m_ready{n}") for n in range(4)]
        s2_mm = sem("s2_mm")
        exp_done = sem("exp_done")
        lo_pool = sem("lo_pool")
        lo_dve = sem("lo_dve")
        pv_mm = sem("pv_mm")
        usum_done = sem("usum_done")
        rden_done = sem("rden_done")
        attn_done = sem("attn_done")
        attnT_mm = sem("attnT_mm")
        attnT_ev = sem("attnT_ev")
        wo_mm = sem("wo_mm")
        x2_done = sem("x2_done")
        bn2 = sem("bn2")
        agg2 = sem("agg2")
        pool2 = sem("pool2")
        xn2_done = sem("xn2_done")
        x2T_mm = sem("x2T_mm")
        x2T_ev = sem("x2T_ev")
        gate_mm = sem("gate_mm")
        gate_ev = sem("gate_ev")
        route = sem("route")
        onehot_done = sem("onehot_done")
        slot_done = sem("slot_done")
        rank_mm = sem("rank_mm")
        block_expert = sem("block_expert")
        scattered = sem("scattered")
        blk_in = [sem(f"blk_in{i}") for i in range(3)]
        w_in = [sem(f"w_in{i}") for i in range(2)]
        bT_mm = sem("bT_mm")
        bT_ev = sem("bT_ev")
        h_mm = sem("h_mm")
        h_act = sem("h_act")
        h_dve = sem("h_dve")
        y_mm = sem("y_mm")
        res_done = sem("res_done")
        out_done = sem("out_done")
        out_sent = [sem(f"out_sent{i}") for i in range(2)]

        TOKS = [slice(c * CT, (c + 1) * CT) for c in range(NC)]

        xbank, qbank = [bankA, bankU], [bankT, bankM]
        kbank, vbank = bankC_[0:2], bankC_[2:4]

        S2_LAG = 3
        PV_LAG = 4
        OUT_LAG = 5
        GATE_LAG = 10
        ROUNDS = NB + OUT_LAG
        NORM_ROUNDS = [CB * (c + 1) + OUT_LAG for c in range(NC - 1)]
        LO_POOL = 12

        def hi_of(p):
            return p.bitcast(BF16).rearrange("p (n two) -> p n two", two=2)[:, :, 1]

        block = ctx.enter_context(nc.Block())

        @block.sync
        def _(sp):
            sp.dma_start(w_sb[:], wqkvoT).then_inc(ld_w, 16)
            for c in range(NC):
                sp.dma_start(x_sb[:, c * CB:(c + 1) * CB, :],
                             x[c * CB:(c + 1) * CB].rearrange("b t d -> t b d")).then_inc(ld_x[c], 16)
                sp.dma_start(ctx_sb[:, TOKS[c]], ctxT[:, TOKS[c]]).then_inc(ld_ctx[c], 16)
                if c == 0:
                    sp.dma_start(cf[:], constf).then_inc(ld_const, 16)
                    sp.dma_start(cols_sb[:], cols).then_inc(ld_small, 16)
                    sp.dma_start(rows_sb[:], rows.partition_broadcast(128)).then_inc(ld_small, 16)
                    sp.dma_start(gains_sb[:], gains.partition_broadcast(128)).then_inc(ld_small, 16)
                    sp.dma_start(gateb_sb[:], gate_b.partition_broadcast(128)).then_inc(ld_small, 16)
                    sp.dma_start(gate_sb[:], gateT).then_inc(ld_small, 16)
                    sp.dma_start(ch[:], consth).then_inc(ld_small, 16)
            for g in range(NG):
                sp.dma_start(k_dram[g, :, 3], onesh[g]).then_inc(ones_in_k, 16)

            def write_k(c):
                sp.wait_ge(k_lo, c + 1)
                for n, part in enumerate((0, 1, 0)):
                    sp.dma_start(k_dram[:, :, n, :, TOKS[c]].rearrange("g i d t -> (g i) d t"),
                                 k_part[:, c % 2, part, :]).then_inc(k_written[c], 16)

            def write_q(c):
                sp.wait_ge(q_lo, c + 1)
                for n, part in enumerate((0, 0, 1)):
                    sp.dma_start(q_dram[:, :, n, :, TOKS[c]].rearrange("g i d t -> (g i) d t"),
                                 q_part[:, c % 2, part, :]).then_inc(q_written[c], 16)

            def read_k(c):
                sp.wait_ge(ones_in_k, 16 * NG)
                sp.wait_ge(k_written[c], 48)
                sp.dma_start(k_st[:, :, TOKS[c]],
                             k_dram[:, :, :, :, TOKS[c]].rearrange("g i n d t -> (i n d) g t")).then_inc(k_ready[c], 16)

            def read_q(c):
                sp.wait_ge(q_zero[c], NG)
                sp.wait_ge(q_written[c], 48)
                for i in range(4):
                    sp.dma_start(q_st[SLOT * i:SLOT * i + 3 * DH, :, i, TOKS[c]],
                                 q_dram[:, i, :, :, TOKS[c]].rearrange("g n d t -> (n d) g t")).then_inc(q_ready[c], 16)

            def send_max(b):
                sp.wait_ge(mT_ev, b + 1)
                sp.dma_start(m_dram[b].rearrange("i n g t -> (i n g) t"), mT[:, b % 2, :]).then_inc(m_written, 16)
                sp.wait_ge(m_written, 16 * (b + 1))
                if b >= 4:
                    sp.wait_ge(m_ready[b % 4], 64 * (b // 4))
                for i in range(4):
                    sp.dma_start(q_st[SLOT * i + 3 * DH:SLOT * i + 3 * DH + 2, :, i, b * T:(b + 1) * T],
                                 m_dram[b, i]).then_inc(m_ready[b % 4], 16)

            for c in range(2):
                write_k(c)
                write_q(c)
                read_k(c)
                read_q(c)
            for c in range(2, NC):
                write_k(c)
                write_q(c)
                read_k(c)
            for b in range(NB):
                send_max(b)
                if b < 2:
                    read_q(2 + b)
                elif b < 2 + NE:
                    e = b - 2
                    sp.dma_start(experts[:, e, 0:W_B2], wexp[e]).then_inc(ld_exp, 16)
                    if e == 0:
                        sp.dma_start(experts[:, :, W_B2:WCOL], b2r.partition_broadcast(128)).then_inc(ld_b2, 16)
                        sp.wait_ge(fill_done, 1)
                    n0, n1 = 3 * e, min(3 * e + 3, NBLK)
                    sp.dma_start(sorted_dram[n0 * 128:n1 * 128, :].rearrange("(n p) w -> p n w", p=128),
                                 fill[:].unsqueeze(1).to_broadcast([128, n1 - n0, ROW])).then_inc(sorted_init, 16)

            sp.wait_ge(block_expert, 2)
            sp.wait_ge(scattered, 16 * NB)
            sp.wait_ge(b2g_done, 1)
            for k in range(NBLK):
                e = sp.value_load(bexp[0:1, k:k + 1], min_val=0, max_val=NE - 1)
                if k >= 3:
                    sp.wait_ge(bT_mm, k - 2)
                    sp.wait_ge(out_sent[(k - 3) % 2], 16 * ((k - 3) // 2 + 1))
                sp.dma_start(blk[:, k % 3, :], sorted_dram[k * 128:(k + 1) * 128, :]).then_inc(blk_in[k % 3], 16)
                if k >= 2:
                    sp.wait_ge(y_mm, k - 1)
                    sp.wait_ge(res_done, k - 1)
                sp.dma_start(wblk[:, k % 2, :], experts[:, bass.ds(e, 1), :]).then_inc(w_in[k % 2], 16)

        @block.gpsimd
        def _(pool):
            pool.memset(v_sb[:, :, :, DH:DH + 1], 1.0).then_inc(v_init, 1)
            pool.memset(v_sb[:, :, :, VC - 1:VC], 0.0).then_inc(v_init, 1)
            pool.memset(fill[:], 1.0).then_inc(fill_done, 1)
            pool.memset(mhalf[:], -0.5).then_inc(pool2, 1)
            pool.memset(ones8[:], 1.0).then_inc(fill_done, 1)

            for g in range(NG):
                pool.memset(q_st[:, g, :, TOKS[1]].bitcast(U32), 0).then_inc(q_zero[1], 1)

            for c in range(NC):
                pool.wait_ge(nmr1, c + 1)
                if c >= 2:
                    pool.wait_ge(xnT_mm, c - 1)
                for j in range(CB):
                    b = c * CB + j
                    pool.tensor_scalar(xn[:, c % 2, j, :], x_sb[:, b, :], rstd[:, b:b + 1], nmr[:, b:b + 1],
                                       ALU.mult, ALU.add).then_inc(xn_done, 1)
                pool.wait_ge(v_hi, c + 1)
                pool.tensor_tensor(v_sb[:, c * CB:(c + 1) * CB, :, DH + 1:VC - 1],
                                   v32[:, c % 2].rearrange("p b (h d) -> p b h d", h=NH),
                                   v_sb[:, c * CB:(c + 1) * CB, :, 0:DH], ALU.subtract).then_inc(v_lo, 1)
            for c in (2, 3):
                for g in range(NG):
                    pool.memset(q_st[:, g, :, TOKS[c]].bitcast(U32), 0).then_inc(q_zero[c], 1)
            pool.wait_ge(ld_small, 96)
            pool.wait_ge(tg_done, 1)
            pool.tensor_scalar(gbo[:], rows_sb[:, 1, :], tg[:, 0:1], 0.0, ALU.mult, ALU.add).then_inc(gbo_done, 1)
            pool.wait_ge(gbo_done, 1)
            pool.wait_ge(xn_done, NB)
            for c in range(NC):
                pool.tensor_tensor(x_sb[:, c * CB:(c + 1) * CB, :], x_sb[:, c * CB:(c + 1) * CB, :],
                                   gbo[:].unsqueeze(1).to_broadcast([128, CB, D]), ALU.add).then_inc(xb_done, 1)

            def lo_part(b, n):
                h0, h1 = ((0, 8), (8, LO_POOL))[n]
                pool.wait_ge(exp_done, 2 * b + n + 1)
                if b >= 2:
                    pool.wait_ge(pv_mm, 4 * (b - 1))
                pool.tensor_tensor(prob_lo[:, b % 2, h0 * T:h1 * T], prob[:, b % 2, h0 * T:h1 * T],
                                   hi_of(prob[:, b % 2, h0 * T:h1 * T]), ALU.subtract).then_inc(lo_pool, 1)

            def norm2(c):
                s = slice(c * CB, (c + 1) * CB)
                pool.wait_ge(agg2, CB * (c + 1))
                pool.tensor_scalar(ve2[:, s], mv2[:, s, 1], 1.0, EPS, ALU.mult, ALU.add).then_inc(pool2, 1)
                pool.wait_ge(pool2, 3 * c + 2)
                pool.tensor_tensor(rstd2[:, s], ve2[:, s], mhalf[:, s], ALU.pow).then_inc(pool2, 1)
                pool.wait_ge(pool2, 3 * c + 3)
                pool.tensor_tensor(nmr2[:, s], mv2[:, s, 0], rstd2[:, s], ALU.mult).then_inc(pool2, 1)
                pool.wait_ge(pool2, 3 * c + 4)
                for b in range(c * CB, (c + 1) * CB):
                    pool.tensor_scalar(token_row[:, b, 0:D], token_row[:, b, D:2 * D], rstd2[:, b:b + 1], nmr2[:, b:b + 1],
                                       ALU.mult, ALU.subtract).then_inc(xn2_done, 1)

            for i in range(S2_LAG, ROUNDS):
                if i - S2_LAG < NB:
                    lo_part(i - S2_LAG, 0)
                if i in NORM_ROUNDS:
                    norm2(NORM_ROUNDS.index(i))
                if i == ROUNDS - 3:
                    pool.wait_ge(ld_b2, 16)
                    pool.tensor_scalar(experts[:, :, W_B2:WCOL], experts[:, :, W_B2:WCOL],
                                       tg[:, 1:2], 0.0, ALU.mult, ALU.add).then_inc(b2g_done, 1)
                if i - S2_LAG < NB:
                    lo_part(i - S2_LAG, 1)
            norm2(NC - 1)

            pool.wait_ge(sorted_init, 16 * NE)
            pool.wait_ge(slot_done, 1)
            pool.wait_ge(xn2_done, NB)
            pool.wait_ge(ids_done, 1)
            for b in range(NB):
                pool.indirect_dma_start(sorted_dram, bass.IndirectOffsetOnAxis(ap=slot[:, b:b + 1], axis=0),
                                        token_row[:, b, :], None, bounds_check=NBLK * 128 - 1,
                                        oob_is_err=False).then_inc(scattered, 16)

            def residual_b2(k):
                pool.wait_ge(blk_in[k % 3], 16 * (k // 3 + 1))
                pool.wait_ge(w_in[k % 2], 16 * (k // 2 + 1))
                if k >= 2:
                    pool.wait_ge(out_done, k - 1)
                pool.tensor_tensor(res[:, k % 2, :], blk[:, k % 3, D:2 * D], wblk[:, k % 2, W_B2:WCOL],
                                   ALU.add).then_inc(res_done, 1)

            def send(k):
                pool.wait_ge(out_done, k + 1)
                pool.indirect_dma_start(out, bass.IndirectOffsetOnAxis(ap=blk[:, k % 3, 2 * D:2 * D + 1].bitcast(U32), axis=0),
                                        outb[:, k % 2, :], None, bounds_check=NTOK - 1,
                                        oob_is_err=False).then_inc(out_sent[k % 2], 16)

            for k in range(NBLK):
                residual_b2(k)
                if k >= 2:
                    send(k - 2)
            send(NBLK - 2)
            send(NBLK - 1)
            pool.wait_ge(out_sent[0], 16 * ((NBLK + 1) // 2))
            pool.wait_ge(out_sent[1], 16 * (NBLK // 2))

        @block.scalar
        def _(act):
            for c in range(NC):
                act.wait_ge(eps1, c + 1)
                act.activation(std[:, c * CB:(c + 1) * CB], ve1[:, c * CB:(c + 1) * CB], ACT.Sqrt).then_inc(std1, 1)
            act.wait_ge(ld_small, 96)
            act.activation(tg[:], gains_sb[:], ACT.Tanh).then_inc(tg_done, 1)
            act.wait_ge(v_init, 2)
            for c in range(NC):
                act.wait_ge(k_mm, c + 1)
                if c >= 2:
                    act.wait_ge(k_written[c - 2], 48)
                act.activation(k_part[:, c % 2, 0, :], kbank[c % 2], ACT.Identity, bias=cols_sb[:, 1:2]).then_inc(k_hi, 1)
                act.wait_ge(xnT_mm, c + 1)
                if c >= 2:
                    act.wait_ge(q_mm, c - 1)
                act.activation(xnT[:, c % 2, :], xbank[c % 2][:], ACT.Copy).then_inc(xnT_ev, 1)
                act.wait_ge(q_mm, c + 1)
                if c >= 2:
                    act.wait_ge(q_written[c - 2], 48)
                act.activation(q_part[:, c % 2, 0, :], qbank[c % 2][:], ACT.Identity, bias=cols_sb[:, 0:1]).then_inc(q_hi, 1)
                act.wait_ge(v_32, c + 1)
                act.activation(v_sb[:, c * CB:(c + 1) * CB, :, 0:DH],
                               v32[:, c % 2].rearrange("p b (h d) -> p b h d", h=NH), ACT.Copy).then_inc(v_hi, 1)

            def exps(b, half):
                act.wait_ge(s2_mm, 4 * b + 2 * half + 2)
                if b >= 2:
                    act.wait_ge(pv_mm, 4 * (b - 1))
                s = slice(half * 1024, half * 1024 + 1024)
                act.activation(prob[:, b % 2, s], bankC[:, s], ACT.Exp, scale=SCALE).then_inc(exp_done, 1)

            def ev_mT(b):
                act.wait_ge(mT_mm, b + 1)
                if b >= 2:
                    act.wait_ge(m_written, 16 * (b - 1))
                act.activation(mT[:, b % 2, :], bankM[0:32, 0:64].bitcast(F16), ACT.Copy).then_inc(mT_ev, 1)

            def ev_attnT(b):
                act.wait_ge(attnT_mm, b + 1)
                if b >= 2:
                    act.wait_ge(wo_mm, b - 1)
                act.activation(attnT[:, b % 2, :], bankT[:, 0:T], ACT.Copy).then_inc(attnT_ev, 1)

            def ev_x2T(b):
                act.wait_ge(x2T_mm, b + 1)
                if b >= 2:
                    act.wait_ge(gate_mm, b - 1)
                act.activation(x2T[:, b % 2, :], bankM[:, 0:T], ACT.Copy).then_inc(x2T_ev, 1)

            for i in range(ROUNDS):
                if 0 <= i - 1 < NB:
                    ev_mT(i - 1)
                if 0 <= i - S2_LAG < NB:
                    exps(i - S2_LAG, 0)
                if i >= GATE_LAG:
                    ev_x2T(i - GATE_LAG)
                if 0 <= i - OUT_LAG < NB:
                    ev_attnT(i - OUT_LAG)
                if 0 <= i - S2_LAG < NB:
                    exps(i - S2_LAG, 1)
            for b in range(ROUNDS - GATE_LAG, NB):
                ev_x2T(b)

            def ev_bT(k):
                act.wait_ge(bT_mm, k + 1)
                if k >= 2:
                    act.wait_ge(h_mm, 2 * (k - 1))
                act.activation(bT[:, k % 2, :], [bankA, bankM][k % 2][:, 0:128], ACT.Copy).then_inc(bT_ev, 1)

            ev_bT(0)
            for k in range(NBLK):
                if k + 1 < NBLK:
                    ev_bT(k + 1)
                act.wait_ge(h_mm, 2 * k + 1)
                act.wait_ge(w_in[k % 2], 16 * (k // 2 + 1))
                if k >= 2:
                    act.wait_ge(y_mm, k - 1)
                for c in range(2):
                    act.activation(hT[:, k % 2, c, :], bankC_[2 * (k % 2)][:, c * 128:c * 128 + 128], ACT.Relu,
                                   bias=wblk[:, k % 2, W_B1 + c:W_B1 + c + 1]).then_inc(h_act, 1)

        @block.vector
        def _(dve):
            def scale1(c):
                s = slice(c * CB, (c + 1) * CB)
                dve.wait_ge(std1, c + 1)
                dve.reciprocal(rstd[:, s], std[:, s]).then_inc(rst1, 1)
                dve.wait_ge(rst1, c + 1)
                dve.scalar_tensor_tensor(nmr[:, s], mv[:, s, 0], -1.0, rstd[:, s], ALU.mult, ALU.mult).then_inc(nmr1, 1)

            for g in range(NG):
                dve.memset(q_st[:, g, :, TOKS[0]].bitcast(U32), 0).then_inc(q_zero[0], 1)
            for c in range(NC):
                s = slice(c * CB, (c + 1) * CB)
                dve.wait_ge(ld_x[c], 16)
                for b in range(c * CB, (c + 1) * CB):
                    dve.bn_stats(stats[:, b, :], x_sb[:, b, :]).then_inc(bn1, 1)
                for b in range(c * CB, (c + 1) * CB):
                    dve.wait_ge(bn1, b + 1)
                    dve.bn_aggr(mv[:, b, :], stats[:, b, :]).then_inc(agg1, 1)
                dve.wait_ge(agg1, CB * (c + 1))
                dve.tensor_scalar(ve1[:, s], mv[:, s, 1], EPS, None, ALU.add).then_inc(eps1, 1)
                if c >= 1:
                    scale1(c - 1)
            scale1(NC - 1)
            dve.wait_ge(ld_small, 96)
            for c in range(NC):
                dve.wait_ge(k_hi, c + 1)
                dve.scalar_tensor_tensor(k_part[:, c % 2, 1, :], kbank[c % 2], cols_sb[:, 1:2], k_part[:, c % 2, 0, :],
                                         ALU.add, ALU.subtract).then_inc(k_lo, 1)
                dve.wait_ge(v_mm, c + 1)
                if c >= 2:
                    dve.wait_ge(v_lo, c - 1)
                dve.tensor_tensor(v32[:, c % 2], vbank[c % 2].rearrange("p (b n) -> p b n", b=CB),
                                  rows_sb[:, 0, :].unsqueeze(1).to_broadcast([128, CB, D]), ALU.add).then_inc(v_32, 1)
                dve.wait_ge(q_hi, c + 1)
                dve.scalar_tensor_tensor(q_part[:, c % 2, 1, :], qbank[c % 2][:], cols_sb[:, 0:1], q_part[:, c % 2, 0, :],
                                         ALU.add, ALU.subtract).then_inc(q_lo, 1)
            dve.wait_ge(ld_const, 16)
            dve.tensor_copy(token_row[:, :, 2 * D:ROW].bitcast(I32),
                            cf[:, C_TOK:C_TOK + NB].unsqueeze(2).to_broadcast([128, NB, ROW - 2 * D])).then_inc(ids_done, 1)

            def rowmax(b, g):
                dve.wait_ge(s1_mm, 4 * b + g + 1)
                if b >= 2 and g == 0:
                    dve.wait_ge(m_lo, b - 1)
                dve.tensor_reduce(mx[:, b % 2, 4 * g:4 * g + 4], bankA[:].rearrange("p (i s) -> p i s", i=4),
                                  axis=AX.X, op=ALU.max).then_inc(max_done, 1)

            def split_max(b):
                m = mx[:, b % 2, :].rearrange("p (g i) -> p i g", g=NG)
                c = mcol[:, b % 2, :].rearrange("p (i n g) -> p i n g", i=4, n=2)
                dve.wait_ge(max_done, 4 * b + 4)
                if b >= 2:
                    dve.wait_ge(mT_mm, b - 1)
                dve.tensor_scalar(c[:, :, 0, :], m, -1.0, None, ALU.mult).then_inc(m_hi, 1)
                dve.wait_ge(m_hi, b + 1)
                dve.scalar_tensor_tensor(c[:, :, 1, :], m, -1.0, c[:, :, 0, :], ALU.mult, ALU.subtract).then_inc(m_lo, 1)

            def lo_part(b):
                s = slice(LO_POOL * T, NH * T)
                dve.wait_ge(exp_done, 2 * b + 2)
                if b >= 2:
                    dve.wait_ge(pv_mm, 4 * (b - 1))
                dve.tensor_tensor(prob_lo[:, b % 2, s], prob[:, b % 2, s], hi_of(prob[:, b % 2, s]),
                                  ALU.subtract).then_inc(lo_dve, 1)

            def normalise(b):
                dve.wait_ge(pv_mm, 4 * (b + 1))
                if b >= 1:
                    dve.wait_ge(attn_done, b)
                u = bankU[:, 0:NH * VC].rearrange("p (h n c) -> p h c n", h=NH, n=2)
                dve.tensor_reduce(usum[:], u, axis=AX.X, op=ALU.add).then_inc(usum_done, 1)
                dve.wait_ge(usum_done, b + 1)
                dve.reciprocal(rden[:], usum[:, :, DH]).then_inc(rden_done, 1)
                dve.wait_ge(rden_done, b + 1)
                if b >= 2:
                    dve.wait_ge(attnT_mm, b - 1)
                dve.tensor_tensor(attn[:, b % 2, :].rearrange("p (h d) -> p h d", h=NH), usum[:, :, 0:DH],
                                  rden[:].unsqueeze(2).to_broadcast([128, NH, DH]), ALU.mult).then_inc(attn_done, 1)

            def residual(b):
                dve.wait_ge(wo_mm, b + 1)
                dve.wait_ge(xb_done, b // CB + 1)
                dve.scalar_tensor_tensor(token_row[:, b, D:2 * D], bankT[:, 128:256], tg[:, 0:1], x_sb[:, b, :],
                                         ALU.mult, ALU.add).then_inc(x2_done, 1)
                dve.wait_ge(x2_done, b + 1)
                dve.bn_stats(stats2[:, b, :], token_row[:, b, D:2 * D]).then_inc(bn2, 1)
                dve.wait_ge(bn2, b + 1)
                dve.bn_aggr(mv2[:, b, :], stats2[:, b, :]).then_inc(agg2, 1)

            def ev_gate(b):
                dve.wait_ge(gate_mm, b + 1)
                dve.tensor_tensor(logit[:, b, :], bankM[:, 128:128 + NE], gateb_sb[:], ALU.add).then_inc(gate_ev, 1)

            for i in range(ROUNDS):
                if 0 <= i - OUT_LAG < NB:
                    normalise(i - OUT_LAG)
                if i < NB:
                    rowmax(i, 0)
                    rowmax(i, 1)
                if 0 <= i - PV_LAG < NB:
                    lo_part(i - PV_LAG)
                if i < NB:
                    rowmax(i, 2)
                    rowmax(i, 3)
                    split_max(i)
                if 0 <= i - OUT_LAG < NB:
                    residual(i - OUT_LAG)
                if i >= GATE_LAG:
                    ev_gate(i - GATE_LAG)
            for b in range(ROUNDS - GATE_LAG, NB):
                ev_gate(b)

            steps = [0]

            def step(ins):
                steps[0] += 1
                ins.then_inc(route, 1)
                dve.wait_ge(route, steps[0])

            dve.wait_ge(gate_ev, NB)
            step(dve.tensor_reduce(lmax[:], logit[:], axis=AX.X, op=ALU.max))
            step(dve.tensor_tensor(isbest[:], logit[:], lmax[:].unsqueeze(2).to_broadcast([128, NB, NE]), ALU.is_equal))
            step(dve.tensor_tensor(wgt[:], isbest[:], cf[:, C_E:C_E + NE].unsqueeze(1).to_broadcast([128, NB, NE]), ALU.mult))
            step(dve.tensor_reduce(wmax[:], wgt[:], axis=AX.X, op=ALU.max))
            dve.tensor_tensor(onehot_h[:], wgt[:], wmax[:].unsqueeze(2).to_broadcast([128, NB, NE]),
                              ALU.is_equal).then_inc(onehot_done, 1)
            dve.wait_ge(rank_mm, 2)
            dve.wait_ge(fill_done, 2)
            step(dve.tensor_tensor(nbc[:], bankA[:, 0:NE].unsqueeze(2).to_broadcast([128, NE, NB]),
                                   cf[:, C_J:C_J + NE * NB].rearrange("p (e j) -> p e j", e=NE), ALU.is_gt))
            step(dve.tensor_reduce(nblk[:], nbc[:], axis=AX.X, op=ALU.add))
            step(dve.tensor_tensor_scan(bend[:], ones8[:], nblk[:], 0.0, ALU.mult, ALU.add))
            step(dve.tensor_tensor(bstart[:], bend[:], nblk[:], ALU.subtract))
            step(dve.scalar_tensor_tensor(base[:], bstart[:].unsqueeze(1).to_broadcast([128, NB, NE]), 128.0,
                                          bankT[:, 0:NB * NE].rearrange("p (b e) -> p b e", b=NB), ALU.mult, ALU.add))
            step(dve.tensor_tensor(picked[:], base[:], onehot_h[:], ALU.mult))
            step(dve.tensor_reduce(slotf[:], picked[:], axis=AX.X, op=ALU.add))
            dve.tensor_copy(slot[:], slotf[:]).then_inc(slot_done, 1)
            step(dve.tensor_tensor(ble[:], bend[:].unsqueeze(1).to_broadcast([128, NBLK, NE]),
                                   cf[:, C_B:C_B + NBLK * NE].rearrange("p (n e) -> p n e", n=NBLK), ALU.is_le))
            step(dve.tensor_reduce(bexpf[:], ble[:], axis=AX.X, op=ALU.add))
            dve.tensor_scalar(bexp[:, 0:NBLK], bexpf[:], float(NE - 1), None, ALU.min).then_inc(block_expert, 2)

            def relu(k):
                dve.wait_ge(h_mm, 2 * k + 2)
                dve.wait_ge(w_in[k % 2], 16 * (k // 2 + 1))
                if k >= 2:
                    dve.wait_ge(y_mm, k - 1)
                for c in range(2, 4):
                    dve.tensor_scalar(hT[:, k % 2, c, :], bankC_[2 * (k % 2) + 1][:, (c - 2) * 128:(c - 1) * 128],
                                      wblk[:, k % 2, W_B1 + c:W_B1 + c + 1], 0.0, ALU.add, ALU.max).then_inc(h_dve, 1)

            def finish(k):
                dve.wait_ge(y_mm, k + 1)
                dve.wait_ge(res_done, k + 1)
                if k >= 2:
                    dve.wait_ge(out_sent[k % 2], 16 * (k // 2))
                dve.scalar_tensor_tensor(outb[:, k % 2, :], [bankU, bankT][k % 2][:, 0:D], tg[:, 1:2], res[:, k % 2, :],
                                         ALU.mult, ALU.add).then_inc(out_done, 1)

            for k in range(NBLK):
                relu(k)
                if k >= 1:
                    finish(k - 1)
            finish(NBLK - 1)

        @block.tensor
        def _(pe):
            pe.wait_ge(ld_w, 16)
            for c in range(NC):
                pe.wait_ge(ld_ctx[c], 16)
                if c >= 2:
                    pe.wait_ge(k_lo, c - 1)
                pe.matmul(kbank[c % 2], w_sb[:, 1, :], ctx_sb[:, TOKS[c]], start=True, stop=True).then_inc(k_mm, 1)
                pe.wait_ge(xn_done, CB * (c + 1))
                pe.wait_ge(ld_const, 16)
                if c >= 2:
                    pe.wait_ge(xnT_ev, c - 1)
                for j in range(CB):
                    ins = pe.transpose(xbank[c % 2][:, j * T:(j + 1) * T], xn[:, c % 2, j, :], ident)
                ins.then_inc(xnT_mm, 1)
                if c >= 2:
                    pe.wait_ge(v_32, c - 1)
                for j in range(CB):
                    b = c * CB + j
                    ins = pe.matmul(vbank[c % 2][:, j * D:(j + 1) * D], ctx_sb[:, b * T:(b + 1) * T], w_sb[:, 2, :],
                                    start=True, stop=True)
                ins.then_inc(v_mm, 1)
                pe.wait_ge(xnT_ev, c + 1)
                if c >= 2:
                    pe.wait_ge(q_lo, c - 1)
                pe.matmul(qbank[c % 2][:], w_sb[:, 0, :], xnT[:, c % 2, :], start=True, stop=True).then_inc(q_mm, 1)

            def scores(b, g):
                pe.wait_ge(max_done, 4 * b + g) if b or g else pe.wait_ge(xnT_ev, NC)
                if g == 0:
                    pe.wait_ge(k_ready[b // CB], 16)
                    pe.wait_ge(q_ready[b // CB], 64)
                for i in range(4):
                    ins = pe.matmul(bankA[:, i * T:(i + 1) * T], q_st[:, g, i, b * T:(b + 1) * T],
                                    k_st[:, g, b * T:(b + 1) * T], start=True, stop=True)
                ins.then_inc(s1_mm, 1)

            def shifted(b, g):
                if g == 0:
                    pe.wait_ge(m_ready[b % 4], 64 * (b // 4 + 1))
                if b >= 1 and g % 2 == 0:
                    pe.wait_ge(exp_done, 2 * b - 1 + g // 2)
                if b == 0 and g == 0:
                    pe.wait_ge(v_32, NC)
                    pe.wait_ge(k_lo, NC)
                    pe.wait_ge(v_lo, NC)
                    pe.wait_ge(v_hi, NC)
                pe.matmul(bankC_[g].rearrange("p (i t) -> p i t", i=4), k_st[:, g, b * T:(b + 1) * T],
                          q_st[:, g, :, b * T:(b + 1) * T], start=True, stop=True).then_inc(s2_mm, 1)

            def times_v(b, g):
                if g == 0:
                    if b >= 1:
                        pe.wait_ge(usum_done, b)
                if g % 2 == 0:
                    pe.wait_ge(exp_done, 2 * b + 1 + g // 2)
                    pe.wait_ge(lo_pool, 2 * b + 1 + g // 2)
                if g == 3:
                    pe.wait_ge(lo_dve, b + 1)
                for h in range(4 * g, 4 * g + 4):
                    u = bankU[:, h * VC:(h + 1) * VC]
                    s = slice(h * T, (h + 1) * T)
                    pe.matmul(u, hi_of(prob[:, b % 2, s]), v_sb[:, b, h, :], start=True, stop=False)
                    ins = pe.matmul(u, prob_lo[:, b % 2, s], v_sb[:, b, h, :], start=False, stop=True)
                ins.then_inc(pv_mm, 1)

            def max_T(b):
                pe.wait_ge(m_lo, b + 1)
                pe.wait_ge(ld_small, 96)
                if b == 0:
                    pe.wait_ge(q_lo, NC)
                else:
                    pe.wait_ge(mT_ev, b)
                if b + 1 > GATE_LAG:
                    pe.wait_ge(gate_ev, b + 1 - GATE_LAG)
                pe.transpose(bankM[0:32, 0:64].bitcast(F16), mcol[:, b % 2, :], ident_h).then_inc(mT_mm, 1)

            def attn_T(b):
                pe.wait_ge(attn_done, b + 1)
                if b >= 1:
                    pe.wait_ge(x2_done, b)
                pe.transpose(bankT[:, 0:T], attn[:, b % 2, :], ident).then_inc(attnT_mm, 1)

            def times_wo(b):
                pe.wait_ge(attnT_ev, b + 1)
                pe.matmul(bankT[:, 128:256], attnT[:, b % 2, :], w_sb[:, 3, :], start=True, stop=True).then_inc(wo_mm, 1)

            def x2_T(b):
                pe.wait_ge(xn2_done, b + 1)
                pe.wait_ge(mT_ev, min(NB, b + GATE_LAG))
                if b >= 1:
                    pe.wait_ge(gate_ev, b)
                pe.transpose(bankM[:, 0:T], token_row[:, b, 0:D], ident).then_inc(x2T_mm, 1)

            def gate(b):
                pe.wait_ge(x2T_ev, b + 1)
                pe.matmul(bankM[:, 128:128 + NE], x2T[:, b % 2, :], gate_sb[:], start=True, stop=True).then_inc(gate_mm, 1)

            for i in range(ROUNDS):
                for g in range(NG):
                    if i < NB:
                        scores(i, g)
                    if 0 <= i - S2_LAG < NB:
                        shifted(i - S2_LAG, g)
                    if g == 0 and 0 <= i - 1 < NB:
                        max_T(i - 1)
                    if 0 <= i - PV_LAG < NB:
                        times_v(i - PV_LAG, g)
                    if g == 1 and 0 <= i - OUT_LAG < NB:
                        attn_T(i - OUT_LAG)
                    if g == 1 and i >= GATE_LAG:
                        x2_T(i - GATE_LAG)
                    if g == 2 and 0 <= i - OUT_LAG < NB:
                        times_wo(i - OUT_LAG)
                    if g == 3 and i >= GATE_LAG:
                        gate(i - GATE_LAG)
            for b in range(ROUNDS - GATE_LAG, NB):
                x2_T(b)
                gate(b)

            pe.wait_ge(onehot_done, 1)
            pe.wait_ge(x2_done, NB)
            oh = onehot_h[:].rearrange("p b e -> p (b e)")
            pe.matmul(bankT[:, 0:NB * NE], before_h, oh, start=True, stop=False)
            for j in range(1, NB):
                ins = pe.matmul(bankT[:, j * NE:NB * NE], ones_h, oh[:, 0:(NB - j) * NE], start=False, stop=(j == NB - 1))
            ins.then_inc(rank_mm, 1)
            pe.wait_ge(max_done, 4 * NB)
            for b in range(NB):
                ins = pe.matmul(bankA[:, 0:NE], ones_h, onehot_h[:, b, :], start=(b == 0), stop=(b == NB - 1))
            ins.then_inc(rank_mm, 1)

            def block_T(k):
                pe.wait_ge(blk_in[k % 3], 16 * (k // 3 + 1))
                if k >= 2:
                    pe.wait_ge(bT_ev, k - 1)
                else:
                    pe.wait_ge(slot_done, 1)
                    pe.wait_ge(gate_ev, NB)
                pe.transpose([bankA, bankM][k % 2][:, 0:128], blk[:, k % 3, 0:D], ident).then_inc(bT_mm, 1)

            def hidden(k):
                pe.wait_ge(bT_ev, k + 1)
                pe.wait_ge(w_in[k % 2], 16 * (k // 2 + 1))
                if k >= 2:
                    pe.wait_ge(h_act, 2 * (k - 1))
                    pe.wait_ge(h_dve, 2 * (k - 1))
                else:
                    pe.wait_ge(exp_done, 2 * NB)
                for half in range(2):
                    for c in range(2):
                        ins = pe.matmul(bankC_[2 * (k % 2) + half][:, c * 128:(c + 1) * 128],
                                        wblk[:, k % 2, (2 * half + c) * 128:(2 * half + c + 1) * 128], bT[:, k % 2, :],
                                        start=True, stop=True)
                    ins.then_inc(h_mm, 1)

            def down(k):
                pe.wait_ge(h_act, 2 * (k + 1))
                pe.wait_ge(h_dve, 2 * (k + 1))
                if k >= 2:
                    pe.wait_ge(out_done, k - 1)
                for c in range(HC):
                    ins = pe.matmul([bankU, bankT][k % 2][:, 0:D], hT[:, k % 2, c, :],
                                    wblk[:, k % 2, W_W2 + c * D:W_W2 + (c + 1) * D], start=(c == 0), stop=(c == HC - 1))
                ins.then_inc(y_mm, 1)

            block_T(0)
            for k in range(NBLK):
                if k + 1 < NBLK:
                    block_T(k + 1)
                hidden(k)
                if k >= 1:
                    down(k - 1)
            down(NBLK - 1)


def kernel(x, ctx_1024, g_xattn, g_ffn, L0_xattn_wq_w, L0_xattn_wq_b, L0_xattn_wk_w, L0_xattn_wk_b, L0_xattn_wv_w,
           L0_xattn_wv_b, L0_xattn_wo_w, L0_xattn_wo_b, L0_ffn_gate_w, L0_ffn_gate_b, L0_ffn_w1, L0_ffn_b1, L0_ffn_w2,
           L0_ffn_b2):
    import numpy as np
    import concourse.bacc as bacc
    from concourse.bass_utils import run_bass_kernel_spmd

    a = {n: np.asarray(v) for n, v in dict(
        x=x, ctx=ctx_1024, gx=g_xattn, gf=g_ffn, wq=L0_xattn_wq_w, wk=L0_xattn_wk_w, wv=L0_xattn_wv_w, wo=L0_xattn_wo_w,
        bq=L0_xattn_wq_b, bk=L0_xattn_wk_b, bv=L0_xattn_wv_b, bo=L0_xattn_wo_b, gw=L0_ffn_gate_w, gb=L0_ffn_gate_b,
        w1=L0_ffn_w1, b1=L0_ffn_b1, w2=L0_ffn_w2, b2=L0_ffn_b2).items()}
    p = np.arange(128)
    constf = np.zeros((128, NCONST), np.float32)
    constf[:, C_ID:C_ID + 128] = np.eye(128)
    constf[:, C_J:C_J + NE * NB] = np.tile(128.0 * np.arange(NB), NE)
    constf[:, C_E:C_E + NE] = NE - np.arange(NE)
    constf[:, C_B:C_B + NBLK * NE] = np.repeat(np.arange(NBLK), NE)
    constf[:, C_TOK:C_TOK + NB] = 128 * np.arange(NB)[None, :] + p[:, None]
    consth = np.concatenate([np.eye(128), p[:, None] < p[None, :], np.ones((128, 128))], 1).astype(np.float16)
    ins = {
        "x": a["x"],
        "ctxT": a["ctx"].transpose(2, 0, 1).reshape(D, NTOK),
        "wqkvoT": np.stack([a[n].T for n in ("wq", "wk", "wv", "wo")], 1),
        "gateT": a["gw"].T,
        "cols": np.stack([a["bq"], a["bk"]], 1),
        "rows": np.stack([a["bv"], a["bo"]]),
        "gate_b": a["gb"],
        "gains": np.concatenate([a["gx"], a["gf"]]),
        "wexp": np.concatenate([
            a["w1"].transpose(0, 2, 1),
            a["w2"].transpose(0, 2, 1).reshape(NE, HC, 128, D).transpose(0, 2, 1, 3).reshape(NE, 128, HC * D),
            a["b1"].reshape(NE, HC, 128).transpose(0, 2, 1)], 2),
        "b2r": a["b2"],
        "constf": constf,
        "consth": consth,
        "onesh": np.ones((NG, 4, DH, NTOK), np.float16),
    }
    ins = {n: np.ascontiguousarray(v) for n, v in ins.items()}
    nc = bacc.Bacc("TRN2", target_bir_lowering=False, num_devices=1)
    aps = {n: nc.dram_tensor("in_" + n, v.shape, mybir.dt.from_np(v.dtype), kind="ExternalInput").ap() for n, v in ins.items()}
    out = nc.dram_tensor("out", (NTOK, D), F32, kind="ExternalOutput").ap()
    program(nc, **aps, out=out)
    r = run_bass_kernel_spmd(nc, [{"in_" + n: v for n, v in ins.items()}], core_ids=[0])
    return r.results[0]["out"].reshape(NB, T, D)
```

```python
import concourse.bass as bass
from concourse import mybir
from contextlib import ExitStack

F32 = mybir.dt.float32
F16 = mybir.dt.float16
BF16 = mybir.dt.bfloat16
I32 = mybir.dt.int32
U32 = mybir.dt.uint32
ALU = mybir.AluOpType
ACT = mybir.ActivationFunctionType
AX = mybir.AxisListType

NB, T, D = 16, 128, 128
NTOK = NB * T
NH, DH = 16, 8
NG = 4
SLOT = 32
NE, HID = 8, 512
HC = HID // 128
NBLK = NTOK // 128 + NE - 1
CB = 4
NC = NB // CB
CT = CB * T
EPS = 1e-5
SCALE = float(DH) ** -0.5
VC = 2 * (DH + 1)
ROW = 2 * D + 8
W_W2, W_B1, W_B2 = HID, HID + HC * D, HID + HC * D + HC
WCOL = W_B2 + D

REGION = NTOK + 128
NROWS = NE * REGION + 128

C_ID = 0
C_W = C_ID + 128
C_GATE = C_W + 4 * D
C_COL = C_GATE + NE
C_J = C_COL + 2
C_E = C_J + NE * NB
C_B = C_E + NE
C_B128 = C_B + NBLK * NE
C_REG = C_B128 + NBLK
C_TOK = C_REG + NE
NCONST = C_TOK + NB
V_BV, V_BO, V_GB, V_GAIN = 0, D, 2 * D, 2 * D + NE
NVEC = V_GAIN + 2

def program(nc, x, ctxT, vecs, wexp, b2r, constf, consth, onesh, out):
    ctx = ExitStack()
    with ctx:
        def sb(name, shape, dt=F32):
            return ctx.enter_context(nc.sbuf_tensor(name, shape, dt))

        def ps(name, shape, dt=F32):
            return ctx.enter_context(nc.psum_tensor(name, shape, dt))

        def sem(name):
            return ctx.enter_context(nc.semaphore(name))

        q_dram = nc.dram_tensor("q_stack", (NG, 4, 3, DH, NTOK), F16).ap()
        k_dram = nc.dram_tensor("k_stack", (NG, 4, 4, DH, NTOK), F16).ap()
        sorted_dram = nc.dram_tensor("sorted_rows", (NROWS, ROW), F32).ap()

        x_sb = sb("x_sb", [128, NB, D])
        ctx_sb = sb("ctx_sb", [128, NTOK])
        vec_sb = sb("vec_sb", [128, NVEC])
        tg = sb("tg", [128, 2])
        cf = sb("cf", [128, NCONST])
        ch = sb("ch", [128, 3 * 128], F16)
        experts = sb("experts", [128, NE, WCOL])
        ident = cf[:, C_ID:C_ID + 128]
        w_sb = cf[:, C_W:C_GATE].rearrange("p (n d) -> p n d", n=4)
        gate_sb = cf[:, C_GATE:C_GATE + NE]
        cols_sb = cf[:, C_COL:C_COL + 2]
        ident_h = ch[:, 0:128]
        before_h = ch[:, 128:256]
        ones_h = ch[:, 256:384]

        stats = sb("stats", [128, NB, 6])
        mv = sb("mv", [128, NB, 2])
        ve1 = sb("ve1", [128, NB])
        std = sb("std", [128, NB])
        rstd = sb("rstd", [128, NB])
        nmr = sb("nmr", [128, NB])
        q_part = sb("q_part", [128, 2, 2, CT], F16)
        k_part = sb("k_part", [128, 2, 2, CT], F16)
        v_sb = sb("v_sb", [128, NB, NH, VC], F16)
        q_st = sb("q_st", [128, NG, 4, NTOK], F16)
        k_st = sb("k_st", [128, NG, NTOK], F16)
        gbo = sb("gbo", [128, D])

        mx = sb("mx", [128, 2, NH])
        mcol = sb("mcol", [128, 2, 32], F16)
        mT = sb("mT", [8, 2, NG, T], F16)
        prob = sb("prob", [128, 2, NH * T])
        xn = prob[:, 0, 0:2 * CT].rearrange("p (n b d) -> p n b d", n=2, b=CB)
        xnT = prob[:, 0, 2 * CT:4 * CT].rearrange("p (n t) -> p n t", n=2)
        v32 = prob[:, 1, 0:2 * CT].rearrange("p (n b d) -> p n b d", n=2, b=CB)
        prob_lo = sb("prob_lo", [128, 2, NH * T], F16)
        usum = sb("usum", [128, NH, DH + 1])
        rden = sb("rden", [128, NH])
        attn = sb("attn", [128, 2, D])
        attnT = sb("attnT", [128, 2, T])
        token_row = sb("token_row", [128, NB, ROW])
        stats2 = sb("stats2", [128, NB, 6])
        mv2 = sb("mv2", [128, NB, 2])
        ve2 = sb("ve2", [128, NB])
        std2 = sb("std2", [128, NB])
        rstd2 = sb("rstd2", [128, NB])
        nmr2 = sb("nmr2", [128, NB])
        x2T = ctx_sb[:, 0:CT]
        logit = sb("logit", [128, NB, NE])

        lmax = sb("lmax", [128, NB])
        isbest = sb("isbest", [128, NB, NE])
        picked = sb("picked", [128, NB, NE])
        wgt = sb("wgt", [128, NB, NE])
        onehot_h = sb("onehot_h", [128, NB, NE], F16)
        base = sb("base", [128, NB, NE])
        wmax = sb("wmax", [128, NB])
        ones8 = sb("ones8", [128, NE])
        nbc = ctx_sb[:, CT:CT + NE * NB].rearrange("p (e j) -> p e j", e=NE)
        ble, bgone = (ctx_sb[:, n * CT:n * CT + NBLK * NE].rearrange("p (n e) -> p n e", n=NBLK) for n in (2, 3))
        nblk = sb("nblk", [128, NE])
        bend = sb("bend", [128, NE])
        slotf = sb("slotf", [128, NB])
        slot = sb("slot", [128, NB], U32)
        bexpf = sb("bexpf", [128, NBLK])
        bgonef = sb("bgonef", [128, NBLK])
        bwithin = sb("bwithin", [128, NBLK])
        browf = sb("browf", [128, NBLK])
        steer = sb("steer", [128, 2 * NBLK + NE], I32)
        fill = sb("fill", [128, ROW])
        NBUF, WBUF, OBUF = 8, 6, 4
        q_words = q_st[:].rearrange("p g i t -> p (g i t)").bitcast(F32)
        taken = [0]

        def over_q(*shape):
            size = 1
            for n in shape:
                size *= n
            at, taken[0] = taken[0], taken[0] + size
            names = "abc"[:len(shape)]
            return q_words[:, at:at + size].rearrange(f"p ({' '.join(names)}) -> p {' '.join(names)}",
                                                      **dict(zip(names, shape)))

        blk = over_q(NBUF, ROW)
        wblk = over_q(WBUF, WCOL)
        bT = over_q(2, 128)
        hT = over_q(2, HC, 128)
        res = over_q(2, D)
        outb = over_q(OBUF, D)

        bankA = [ps(f"bankA{n}", [128, 512]) for n in range(2)]
        bankC = ps("bankC", [128, 4 * 512])
        bankU = ps("bankU", [128, 512])
        bankX = ps("bankX", [128, 512])
        bankC_ = [bankC[:, 512 * i:512 * i + 512] for i in range(4)]

        ld_const, ld_half, ld_vec, ld_exp, ld_b2 = (sem(n) for n in ("ld_const", "ld_half", "ld_vec", "ld_exp", "ld_b2"))
        ld_x = [sem(f"ld_x{c}") for c in range(NC)]
        ld_ctx = [sem(f"ld_ctx{c}") for c in range(NC)]
        q_zero = [sem(f"q_zero{c}") for c in range(NC)]
        ones_in_k, v_init, fill_done, ids_done = (sem(n) for n in ("ones_in_k", "v_init", "fill_done", "ids_done"))
        bn1, agg1, eps1, std1, rst1, nmr1, xn_done = (
            sem(n) for n in ("bn1", "agg1", "eps1", "std1", "rst1", "nmr1", "xn_done"))
        xnT_mm, xnT_ev, q_mm, k_mm, v_mm = (sem(n) for n in ("xnT_mm", "xnT_ev", "q_mm", "k_mm", "v_mm"))
        q_hi, q_lo, k_hi, k_lo, v_32, v_hi, v_lo = (
            sem(n) for n in ("q_hi", "q_lo", "k_hi", "k_lo", "v_32", "v_hi", "v_lo"))
        q_written = [sem(f"q_written{c}") for c in range(NC)]
        k_written = [sem(f"k_written{c}") for c in range(NC)]
        q_ready = [sem(f"q_ready{c}") for c in range(NC)]
        k_ready = [sem(f"k_ready{c}") for c in range(NC)]
        tg_done, gbo_done, xb_done, b2g_done = (sem(n) for n in ("tg_done", "gbo_done", "xb_done", "b2g_done"))

        s1_mm, max_done, m_hi, m_lo, mT_mm, mT_ev = (
            sem(n) for n in ("s1_mm", "max_done", "m_hi", "m_lo", "mT_mm", "mT_ev"))
        m_ready = [sem(f"m_ready{n}") for n in range(4)]
        s2_mm, exp_done, lo_pool, lo_dve, pv_mm = (
            sem(n) for n in ("s2_mm", "exp_done", "lo_pool", "lo_dve", "pv_mm"))
        usum_done, rden_done, attn_done, attnT_mm, attnT_ev, wo_mm, x2_done = (
            sem(n) for n in ("usum_done", "rden_done", "attn_done", "attnT_mm", "attnT_ev", "wo_mm", "x2_done"))
        bn2, agg2, eps2, std2_done, rst2, nmr2_done, xn2_act, xn2_dve = (
            sem(n) for n in ("bn2", "agg2", "eps2", "std2_done", "rst2", "nmr2_done", "xn2_act", "xn2_dve"))
        x2T_mm, x2T_ev, gate_mm, gate_ev = (sem(n) for n in ("x2T_mm", "x2T_ev", "gate_mm", "gate_ev"))
        route, onehot_done, rank_mm, base_done, slot_done, count_mm, pad_rows, block_rows = (
            sem(n) for n in ("route", "onehot_done", "rank_mm", "base_done", "slot_done", "count_mm", "pad_rows", "block_rows"))
        scattered, spare_init, padded = (sem(n) for n in ("scattered", "spare_init", "padded"))
        blk_in = [sem(f"blk_in{n}") for n in range(NBUF)]
        w_in = [sem(f"w_in{n}") for n in range(WBUF)]
        bT_mm, bT_ev, h_mm, h_act, h_dve, y_mm, res_done, out_done = (
            sem(n) for n in ("bT_mm", "bT_ev", "h_mm", "h_act", "h_dve", "y_mm", "res_done", "out_done"))
        out_sent = [sem(f"out_sent{n}") for n in range(OBUF)]

        TOKS = [slice(c * CT, (c + 1) * CT) for c in range(NC)]

        xbank, qbank = bankA, [bankU, bankX]
        kbank, vbank = bankC_[0:2], bankC_[2:4]

        S2_LAG = 3
        PV_LAG = 4
        OUT_LAG = 5
        ROUNDS = NB + OUT_LAG
        NORM2 = {13: (0, 2), 17: (2, 3)}
        GATES = {15: 0, 16: 1, 19: 2}

        def ended(i, lag):
            return sum(r + lag < i for r in GATES)

        LO_POOL = 14

        LAST = NB - CB

        def of_act(b):
            return b + 1 if b < LAST else LAST + (b - LAST) // 2 + 1

        def of_dve(b):
            return 0 if b < LAST else (b - LAST + 1) // 2

        def hi_of(p):
            return p.bitcast(BF16).rearrange("p (n two) -> p n two", two=2)[:, :, 1]

        block = ctx.enter_context(nc.Block())

        @block.sync
        def _(sp):
            def load_x(c):
                sp.dma_start(x_sb[:, c * CB:(c + 1) * CB, :],
                             x[c * CB:(c + 1) * CB].rearrange("b t d -> t b d")).then_inc(ld_x[c], 16)

            def load_ctx(c):
                sp.dma_start(ctx_sb[:, TOKS[c]], ctxT[:, TOKS[c]]).then_inc(ld_ctx[c], 16)

            load_x(0)
            sp.dma_start(cf[:], constf).then_inc(ld_const, 16)
            load_ctx(0)
            load_x(1)
            sp.dma_start(vec_sb[:], vecs.partition_broadcast(128)).then_inc(ld_vec, 16)
            load_x(2)
            load_x(3)
            load_ctx(1)
            load_ctx(2)
            load_ctx(3)
            for g in range(NG):
                sp.dma_start(k_dram[g, :, 3], onesh[g]).then_inc(ones_in_k, 16)
            sp.dma_start(ch[:], consth).then_inc(ld_half, 16)

            def write_k(c):
                for n, (part, made) in enumerate(((0, k_hi), (1, k_lo), (0, k_hi))):
                    sp.wait_ge(made, c + 1)
                    sp.dma_start(k_dram[:, :, n, :, TOKS[c]].rearrange("g i d t -> (g i) d t"),
                                 k_part[:, c % 2, part, :]).then_inc(k_written[c], 16)

            def write_q(c):
                for n, (part, made) in enumerate(((0, q_hi), (0, q_hi), (1, q_lo))):
                    sp.wait_ge(made, c + 1)
                    sp.dma_start(q_dram[:, :, n, :, TOKS[c]].rearrange("g i d t -> (g i) d t"),
                                 q_part[:, c % 2, part, :]).then_inc(q_written[c], 16)

            def read_k(c):
                sp.wait_ge(ones_in_k, 16 * NG)
                sp.wait_ge(k_written[c], 48)
                sp.dma_start(k_st[:, :, TOKS[c]],
                             k_dram[:, :, :, :, TOKS[c]].rearrange("g i n d t -> (i n d) g t")).then_inc(k_ready[c], 16)

            def read_q(c):
                sp.wait_ge(q_zero[c], NG)
                sp.wait_ge(q_written[c], 48)
                for i in range(4):
                    sp.dma_start(q_st[SLOT * i:SLOT * i + 3 * DH, :, i, TOKS[c]],
                                 q_dram[:, i, :, :, TOKS[c]].rearrange("g n d t -> (n d) g t")).then_inc(q_ready[c], 16)

            def send_max(b):
                sp.wait_ge(mT_ev, b + 1)
                if b >= 4:
                    sp.wait_ge(m_ready[b % 4], 64 * (b // 4))
                for i in range(4):
                    sp.dma_start(q_st[SLOT * i + 3 * DH:SLOT * i + 3 * DH + 2, :, i, b * T:(b + 1) * T],
                                 mT[2 * i:2 * i + 2, b % 2]).then_inc(m_ready[b % 4], 16)

            write_k(0)
            write_q(0)
            read_k(0)
            read_q(0)
            for c in range(1, NC):
                write_k(c)
                write_q(c)
                read_k(c)
                if c == 1:
                    read_q(c)
            for b in range(NB):
                send_max(b)
                if b < 2:
                    read_q(2 + b)
                elif b < 2 + NE:
                    e = b - 2
                    sp.dma_start(experts[:, e, 0:W_B2], wexp[e]).then_inc(ld_exp, 16)
                    if e == 0:
                        sp.dma_start(experts[:, :, W_B2:WCOL], b2r.partition_broadcast(128)).then_inc(ld_b2, 16)
                        sp.wait_ge(fill_done, 1)
                        sp.dma_start(sorted_dram[NE * REGION:NROWS, :], fill[:]).then_inc(spare_init, 16)

            sp.wait_ge(ld_exp, 16 * NE)
            sp.wait_ge(b2g_done, 1)
            sp.wait_ge(block_rows, 2)

            def load_weights(k):
                e = sp.value_load(steer[0:1, k:k + 1], min_val=0, max_val=NE - 1)
                if k >= WBUF:
                    sp.wait_ge(y_mm, k - WBUF + 1)
                    sp.wait_ge(res_done, k - WBUF + 1)
                sp.dma_start(wblk[:, k % WBUF, :], experts[:, bass.ds(e, 1), :]).then_inc(w_in[k % WBUF], 16)

            def load_block(k):
                row = sp.value_load(steer[0:1, NBLK + k:NBLK + k + 1], min_val=0, max_val=NE * REGION)
                if k >= NBUF:
                    sp.wait_ge(bT_mm, k - NBUF + 1)
                    sp.wait_ge(out_sent[(k - NBUF) % OBUF], 16 * ((k - NBUF) // OBUF + 1))
                sp.dma_start(blk[:, k % NBUF, :], sorted_dram[bass.ds(row, 128), :]).then_inc(blk_in[k % NBUF], 16)

            BLOCKS_AHEAD, WEIGHTS_AHEAD = 4, 3
            for k in range(WEIGHTS_AHEAD):
                load_weights(k)
            sp.wait_ge(spare_init, 16)
            sp.wait_ge(padded, 16 * NE)
            sp.wait_ge(scattered, 16 * NB)
            for k in range(BLOCKS_AHEAD):
                load_block(k)
            for k in range(NBLK):
                if k + BLOCKS_AHEAD < NBLK:
                    load_block(k + BLOCKS_AHEAD)
                if k + WEIGHTS_AHEAD < NBLK:
                    load_weights(k + WEIGHTS_AHEAD)

        @block.gpsimd
        def _(pool):
            pool.memset(v_sb[:, :, :, DH:DH + 1], 1.0).then_inc(v_init, 1)
            pool.memset(v_sb[:, :, :, VC - 1:VC], 0.0).then_inc(v_init, 1)
            pool.memset(fill[:], 1.0).then_inc(fill_done, 1)
            pool.memset(ones8[:], 1.0).then_inc(fill_done, 1)

            def zero_q(c):
                for g in range(NG):
                    pool.memset(q_st[:, g, :, TOKS[c]].bitcast(U32), 0).then_inc(q_zero[c], 1)

            def norm1(c):
                pool.wait_ge(nmr1, c + 1)
                if c >= 2:
                    pool.wait_ge(xnT_mm, c - 1)
                for b in range(c * CB, (c + 1) * CB):
                    pool.tensor_scalar(xn[:, c % 2, b % CB, :], x_sb[:, b, :], rstd[:, b:b + 1], nmr[:, b:b + 1],
                                       ALU.mult, ALU.add).then_inc(xn_done, 1)

            def v_lo_part(c):
                pool.wait_ge(v_hi, c + 1)
                pool.tensor_tensor(v_sb[:, c * CB:(c + 1) * CB, :, DH + 1:VC - 1],
                                   v32[:, c % 2].rearrange("p b (h d) -> p b h d", h=NH),
                                   v_sb[:, c * CB:(c + 1) * CB, :, 0:DH], ALU.subtract).then_inc(v_lo, 1)

            norm1(0)
            norm1(1)
            v_lo_part(0)
            norm1(2)
            v_lo_part(1)
            norm1(3)
            zero_q(1)
            v_lo_part(2)
            v_lo_part(3)
            zero_q(2)
            zero_q(3)
            pool.wait_ge(ld_vec, 16)
            pool.wait_ge(tg_done, 1)
            pool.tensor_scalar(gbo[:], vec_sb[:, V_BO:V_BO + D], tg[:, 0:1], 0.0, ALU.mult, ALU.add).then_inc(gbo_done, 1)
            pool.wait_ge(gbo_done, 1)
            pool.wait_ge(xn_done, NB)
            for c in range(NC):
                pool.tensor_tensor(x_sb[:, c * CB:(c + 1) * CB, :], x_sb[:, c * CB:(c + 1) * CB, :],
                                   gbo[:].unsqueeze(1).to_broadcast([128, CB, D]), ALU.add).then_inc(xb_done, 1)

            def lo_part(b, n):
                h0, h1 = ((0, 8), (8, LO_POOL))[n]
                pool.wait_ge(exp_done, 2 * b + n + 1)
                if b >= 2:
                    pool.wait_ge(pv_mm, 4 * (b - 1))
                pool.tensor_tensor(prob_lo[:, b % 2, h0 * T:h1 * T], prob[:, b % 2, h0 * T:h1 * T],
                                   hi_of(prob[:, b % 2, h0 * T:h1 * T]), ALU.subtract).then_inc(lo_pool, 1)

            for b in range(NB):
                lo_part(b, 0)
                lo_part(b, 1)
            pool.wait_ge(ld_b2, 16)
            pool.tensor_scalar(experts[:, :, W_B2:WCOL], experts[:, :, W_B2:WCOL],
                               tg[:, 1:2], 0.0, ALU.mult, ALU.add).then_inc(b2g_done, 1)
            pool.wait_ge(ids_done, 1)
            for b in range(NB):
                pool.wait_ge(slot_done, b // CB + 1)
                pool.wait_ge(xn2_act, of_act(b))
                if of_dve(b):
                    pool.wait_ge(xn2_dve, of_dve(b))
                pool.indirect_dma_start(sorted_dram, bass.IndirectOffsetOnAxis(ap=slot[:, b:b + 1], axis=0),
                                        token_row[:, b, :], None, bounds_check=NROWS - 1,
                                        oob_is_err=False).then_inc(scattered, 16)

            def residual_b2(k):
                pool.wait_ge(blk_in[k % NBUF], 16 * (k // NBUF + 1))
                pool.wait_ge(w_in[k % WBUF], 16 * (k // WBUF + 1))
                if k >= 2:
                    pool.wait_ge(out_done, k - 1)
                pool.tensor_tensor(res[:, k % 2, :], blk[:, k % NBUF, D:2 * D], wblk[:, k % WBUF, W_B2:WCOL],
                                   ALU.add).then_inc(res_done, 1)

            def send(k):
                pool.wait_ge(out_done, k + 1)
                pool.indirect_dma_start(out, bass.IndirectOffsetOnAxis(ap=blk[:, k % NBUF, 2 * D:2 * D + 1].bitcast(U32), axis=0),
                                        outb[:, k % OBUF, :], None, bounds_check=NTOK - 1,
                                        oob_is_err=False).then_inc(out_sent[k % OBUF], 16)

            for k in range(NBLK):
                residual_b2(k)
                if k >= 2:
                    send(k - 2)
            send(NBLK - 2)
            send(NBLK - 1)
            for n in range(OBUF):
                pool.wait_ge(out_sent[n], 16 * ((NBLK - 1 - n) // OBUF + 1))

        @block.scalar
        def _(act):
            for c in range(NC):
                act.wait_ge(eps1, c + 1)
                act.activation(std[:, c * CB:(c + 1) * CB], ve1[:, c * CB:(c + 1) * CB], ACT.Sqrt).then_inc(std1, 1)
            act.wait_ge(ld_vec, 16)
            act.activation(tg[:], vec_sb[:, V_GAIN:V_GAIN + 2], ACT.Tanh).then_inc(tg_done, 1)
            act.wait_ge(v_init, 2)
            act.wait_ge(ld_const, 16)

            def k_hi_part(c):
                act.wait_ge(k_mm, c + 1)
                if c >= 2:
                    act.wait_ge(k_written[c - 2], 48)
                act.activation(k_part[:, c % 2, 0, :], kbank[c % 2], ACT.Identity, bias=cols_sb[:, 1:2]).then_inc(k_hi, 1)

            k_hi_part(0)
            for c in range(NC):
                act.wait_ge(xnT_mm, c + 1)
                if c >= 2:
                    act.wait_ge(q_mm, c - 1)
                act.activation(xnT[:, c % 2, :], xbank[c % 2][:], ACT.Copy).then_inc(xnT_ev, 1)
                act.wait_ge(v_32, c + 1)
                act.activation(v_sb[:, c * CB:(c + 1) * CB, :, 0:DH],
                               v32[:, c % 2].rearrange("p b (h d) -> p b h d", h=NH), ACT.Copy).then_inc(v_hi, 1)
                act.wait_ge(q_mm, c + 1)
                if c >= 2:
                    act.wait_ge(q_written[c - 2], 48)
                act.activation(q_part[:, c % 2, 0, :], qbank[c % 2][:], ACT.Identity, bias=cols_sb[:, 0:1]).then_inc(q_hi, 1)
                if c + 1 < NC:
                    k_hi_part(c + 1)

            def exps(b, half):
                act.wait_ge(s2_mm, 4 * b + 2 * half + 2)
                if b >= 2:
                    act.wait_ge(pv_mm, 4 * (b - 1))
                s = slice(half * 1024, half * 1024 + 1024)
                act.activation(prob[:, b % 2, s], bankC[:, s], ACT.Exp, scale=SCALE).then_inc(exp_done, 1)

            def ev_mT(b):
                act.wait_ge(mT_mm, b + 1)
                if b >= 2:
                    act.wait_ge(m_ready[(b - 2) % 4], 64 * ((b - 2) // 4 + 1))
                act.activation(mT[:, b % 2].rearrange("p g t -> p (g t)"), bankX[0:8, 0:256].bitcast(F16), ACT.Copy).then_inc(mT_ev, 1)

            def ev_attnT(b):
                act.wait_ge(attnT_mm, b + 1)
                if b >= 2:
                    act.wait_ge(wo_mm, b - 1)
                act.activation(attnT[:, b % 2, :], bankX[:, 0:T], ACT.Copy).then_inc(attnT_ev, 1)

            def std_x2(n, c0, c1):
                act.wait_ge(eps2, n + 1)
                act.activation(std2[:, c0 * CB:c1 * CB], ve2[:, c0 * CB:c1 * CB], ACT.Sqrt).then_inc(std2_done, 1)

            def norm2(n, batches):
                act.wait_ge(nmr2_done, n + 1)
                for b in batches:
                    act.activation(token_row[:, b, 0:D], token_row[:, b, D:2 * D], ACT.Identity,
                                   bias=nmr2[:, b:b + 1], scale=rstd2[:, b:b + 1]).then_inc(xn2_act, 1)

            def ev_x2T(c):
                act.wait_ge(x2T_mm, c + 1)
                if c >= 1:
                    act.wait_ge(gate_mm, c)
                act.activation(x2T, bankX[:], ACT.Copy).then_inc(x2T_ev, 1)

            n = 0
            for i in range(ROUNDS):
                if 0 <= i - 1 < NB:
                    ev_mT(i - 1)
                if 0 <= i - S2_LAG < NB:
                    exps(i - S2_LAG, 0)
                if 0 <= i - OUT_LAG < NB:
                    ev_attnT(i - OUT_LAG)
                if 0 <= i - S2_LAG < NB:
                    exps(i - S2_LAG, 1)
                if i in NORM2:
                    std_x2(n, *NORM2[i])
                    n += 1
                if i - 1 in NORM2:
                    c0, c1 = NORM2[i - 1]
                    norm2(n - 1, range(c0 * CB, c1 * CB))
                if i in GATES:
                    ev_x2T(GATES[i])
            std_x2(n, NC - 1, NC)
            norm2(n, range(LAST, NB, 2))
            ev_x2T(NC - 1)

            act.wait_ge(pad_rows, 1)
            act.wait_ge(fill_done, 1)
            for e in range(NE):
                row = act.value_load(steer[0:1, 2 * NBLK + e:2 * NBLK + e + 1], min_val=e * REGION, max_val=e * REGION + NTOK)
                act.dma_start(sorted_dram[bass.ds(row, 128), :], fill[:]).then_inc(padded, 16)

            def ev_bT(k):
                act.wait_ge(bT_mm, k + 1)
                if k >= 2:
                    act.wait_ge(h_mm, 2 * (k - 1))
                act.activation(bT[:, k % 2, :], bankA[k % 2][:, 0:128], ACT.Copy).then_inc(bT_ev, 1)

            ev_bT(0)
            for k in range(NBLK):
                if k + 1 < NBLK:
                    ev_bT(k + 1)
                act.wait_ge(h_mm, 2 * k + 1)
                act.wait_ge(w_in[k % WBUF], 16 * (k // WBUF + 1))
                if k >= 2:
                    act.wait_ge(y_mm, k - 1)
                for c in range(2):
                    act.activation(hT[:, k % 2, c, :], bankC_[2 * (k % 2)][:, c * 128:c * 128 + 128], ACT.Relu,
                                   bias=wblk[:, k % WBUF, W_B1 + c:W_B1 + c + 1]).then_inc(h_act, 1)

        @block.vector
        def _(dve):
            def scale1(c):
                s = slice(c * CB, (c + 1) * CB)
                dve.wait_ge(std1, c + 1)
                dve.reciprocal(rstd[:, s], std[:, s]).then_inc(rst1, 1)
                dve.wait_ge(rst1, c + 1)
                dve.scalar_tensor_tensor(nmr[:, s], mv[:, s, 0], -1.0, rstd[:, s], ALU.mult, ALU.mult).then_inc(nmr1, 1)

            for g in range(NG - 1):
                dve.memset(q_st[:, g, :, TOKS[0]].bitcast(U32), 0).then_inc(q_zero[0], 1)
            for c in range(NC):
                s = slice(c * CB, (c + 1) * CB)
                dve.wait_ge(ld_x[c], 16)
                for b in range(c * CB, (c + 1) * CB):
                    dve.bn_stats(stats[:, b, :], x_sb[:, b, :]).then_inc(bn1, 1)
                for b in range(c * CB, (c + 1) * CB):
                    dve.wait_ge(bn1, b + 1)
                    dve.bn_aggr(mv[:, b, :], stats[:, b, :]).then_inc(agg1, 1)
                if c >= 1:
                    scale1(c - 1)
                dve.wait_ge(agg1, CB * (c + 1))
                dve.tensor_scalar(ve1[:, s], mv[:, s, 1], EPS, None, ALU.add).then_inc(eps1, 1)
            scale1(NC - 1)
            dve.memset(q_st[:, NG - 1, :, TOKS[0]].bitcast(U32), 0).then_inc(q_zero[0], 1)
            dve.wait_ge(ld_vec, 16)
            dve.wait_ge(ld_const, 16)
            for c in range(NC):
                dve.wait_ge(k_hi, c + 1)
                dve.scalar_tensor_tensor(k_part[:, c % 2, 1, :], kbank[c % 2], cols_sb[:, 1:2], k_part[:, c % 2, 0, :],
                                         ALU.add, ALU.subtract).then_inc(k_lo, 1)
                dve.wait_ge(v_mm, c + 1)
                if c >= 2:
                    dve.wait_ge(v_lo, c - 1)
                dve.tensor_tensor(v32[:, c % 2], vbank[c % 2].rearrange("p (b n) -> p b n", b=CB),
                                  vec_sb[:, V_BV:V_BV + D].unsqueeze(1).to_broadcast([128, CB, D]), ALU.add).then_inc(v_32, 1)
                dve.wait_ge(q_hi, c + 1)
                dve.scalar_tensor_tensor(q_part[:, c % 2, 1, :], qbank[c % 2][:], cols_sb[:, 0:1], q_part[:, c % 2, 0, :],
                                         ALU.add, ALU.subtract).then_inc(q_lo, 1)
            dve.tensor_copy(token_row[:, :, 2 * D:ROW].bitcast(I32),
                            cf[:, C_TOK:C_TOK + NB].unsqueeze(2).to_broadcast([128, NB, ROW - 2 * D])).then_inc(ids_done, 1)

            def rowmax(b, g):
                dve.wait_ge(s1_mm, 4 * b + g + 1)
                if b >= 2 and g == 0:
                    dve.wait_ge(m_lo, b - 1)
                dve.tensor_reduce(mx[:, b % 2, 4 * g:4 * g + 4], bankA[g % 2][:].rearrange("p (i s) -> p i s", i=4),
                                  axis=AX.X, op=ALU.max).then_inc(max_done, 1)

            def max_parts(b, n):
                m = mx[:, b % 2, :].rearrange("p (g i) -> p g i", g=NG)
                c = mcol[:, b % 2, :].rearrange("p (g i n) -> p g i n", g=NG, n=2)
                if n == 0:
                    dve.wait_ge(max_done, 4 * b + 4)
                    if b >= 2:
                        dve.wait_ge(mT_mm, b - 1)
                    dve.tensor_scalar(c[:, :, :, 0], m, -1.0, None, ALU.mult).then_inc(m_hi, 1)
                else:
                    dve.wait_ge(m_hi, b + 1)
                    dve.scalar_tensor_tensor(c[:, :, :, 1], m, -1.0, c[:, :, :, 0], ALU.mult, ALU.subtract).then_inc(m_lo, 1)

            def lo_part(b):
                s = slice(LO_POOL * T, NH * T)
                dve.wait_ge(exp_done, 2 * b + 2)
                if b >= 2:
                    dve.wait_ge(pv_mm, 4 * (b - 1))
                dve.tensor_tensor(prob_lo[:, b % 2, s], prob[:, b % 2, s], hi_of(prob[:, b % 2, s]),
                                  ALU.subtract).then_inc(lo_dve, 1)

            def sum_parts(b):
                dve.wait_ge(pv_mm, 4 * (b + 1))
                if b >= 1:
                    dve.wait_ge(attn_done, b)
                u = bankU[:, 0:NH * VC].rearrange("p (h n c) -> p h c n", h=NH, n=2)
                dve.tensor_reduce(usum[:], u, axis=AX.X, op=ALU.add).then_inc(usum_done, 1)

            def invert(b):
                dve.wait_ge(usum_done, b + 1)
                dve.reciprocal(rden[:], usum[:, :, DH]).then_inc(rden_done, 1)

            def normalise(b):
                dve.wait_ge(rden_done, b + 1)
                if b >= 2:
                    dve.wait_ge(attnT_mm, b - 1)
                dve.tensor_tensor(attn[:, b % 2, :].rearrange("p (h d) -> p h d", h=NH), usum[:, :, 0:DH],
                                  rden[:].unsqueeze(2).to_broadcast([128, NH, DH]), ALU.mult).then_inc(attn_done, 1)

            def residual(b):
                dve.wait_ge(wo_mm, b + 1)
                dve.wait_ge(xb_done, b // CB + 1)
                dve.scalar_tensor_tensor(token_row[:, b, D:2 * D], bankX[:, 128:256], tg[:, 0:1], x_sb[:, b, :],
                                         ALU.mult, ALU.add).then_inc(x2_done, 1)

            def stats_x2(b):
                dve.wait_ge(x2_done, b + 1)
                dve.bn_stats(stats2[:, b, :], token_row[:, b, D:2 * D]).then_inc(bn2, 1)

            def aggr_x2(b):
                dve.wait_ge(bn2, b + 1)
                dve.bn_aggr(mv2[:, b, :], stats2[:, b, :]).then_inc(agg2, 1)

            def eps_x2(c0, c1):
                dve.wait_ge(agg2, c1 * CB)
                dve.tensor_scalar(ve2[:, c0 * CB:c1 * CB], mv2[:, c0 * CB:c1 * CB, 1], EPS, None, ALU.add).then_inc(eps2, 1)

            def scale_x2(n, c0, c1):
                s = slice(c0 * CB, c1 * CB)
                dve.wait_ge(std2_done, n + 1)
                dve.reciprocal(rstd2[:, s], std2[:, s]).then_inc(rst2, 1)
                dve.wait_ge(rst2, n + 1)
                dve.scalar_tensor_tensor(nmr2[:, s], mv2[:, s, 0], -1.0, rstd2[:, s], ALU.mult, ALU.mult).then_inc(nmr2_done, 1)

            def ev_gate(c):
                dve.wait_ge(gate_mm, c + 1)
                dve.tensor_tensor(logit[:, c * CB:(c + 1) * CB, :],
                                  bankX[:, 0:CB * NE].rearrange("p (b e) -> p b e", b=CB),
                                  vec_sb[:, V_GB:V_GB + NE].unsqueeze(1).to_broadcast([128, CB, NE]), ALU.add).then_inc(gate_ev, 1)

            steps = [0]

            def step(ins):
                steps[0] += 1
                ins.then_inc(route, 1)
                dve.wait_ge(route, steps[0])

            def choose(c):
                s = slice(c * CB, (c + 1) * CB)

                def wide(a):
                    return a.unsqueeze(2).to_broadcast([128, CB, NE])
                dve.wait_ge(gate_ev, c + 1)
                step(dve.tensor_reduce(lmax[:, s], logit[:, s], axis=AX.X, op=ALU.max))
                step(dve.tensor_tensor(isbest[:, s], logit[:, s], wide(lmax[:, s]), ALU.is_equal))
                step(dve.tensor_tensor(wgt[:, s], isbest[:, s], cf[:, C_E:C_E + NE].unsqueeze(1).to_broadcast([128, CB, NE]),
                                       ALU.mult))
                step(dve.tensor_reduce(wmax[:, s], wgt[:, s], axis=AX.X, op=ALU.max))
                dve.tensor_tensor(onehot_h[:, s], wgt[:, s], wide(wmax[:, s]), ALU.is_equal).then_inc(onehot_done, 1)

            def place(c):
                s = slice(c * CB, (c + 1) * CB)
                dve.wait_ge(onehot_done, c + 1)
                dve.wait_ge(rank_mm, c + 1)
                dve.tensor_tensor(base[:, s], bankX[:, 0:CB * NE].rearrange("p (b e) -> p b e", b=CB),
                                  cf[:, C_REG:C_REG + NE].unsqueeze(1).to_broadcast([128, CB, NE]), ALU.add).then_inc(base_done, 1)
                dve.wait_ge(base_done, c + 1)
                step(dve.tensor_tensor(picked[:, s], base[:, s], onehot_h[:, s], ALU.mult))
                step(dve.tensor_reduce(slotf[:, s], picked[:, s], axis=AX.X, op=ALU.add))
                dve.tensor_copy(slot[:, s], slotf[:, s]).then_inc(slot_done, 1)

            n = 0
            for i in range(ROUNDS):
                now, out_b = i < NB, i - OUT_LAG
                if out_b >= 0:
                    sum_parts(out_b)
                if 0 <= i - 1 < NB:
                    max_parts(i - 1, 0)
                if now:
                    rowmax(i, 0)
                if out_b >= 0:
                    invert(out_b)
                if 0 <= i - 1 < NB:
                    max_parts(i - 1, 1)
                if now:
                    rowmax(i, 1)
                if out_b >= 0:
                    normalise(out_b)
                if out_b >= 1:
                    stats_x2(out_b - 1)
                if i - 1 in NORM2:
                    scale_x2(n, *NORM2[i - 1])
                    n += 1
                if now:
                    rowmax(i, 2)
                if 0 <= i - PV_LAG < NB:
                    lo_part(i - PV_LAG)
                if out_b >= 1:
                    aggr_x2(out_b - 1)
                if now:
                    rowmax(i, 3)
                if out_b >= 0:
                    residual(out_b)
                if i in NORM2:
                    eps_x2(*NORM2[i])
                if i - 1 in GATES:
                    ev_gate(GATES[i - 1])
                if i - 2 in GATES:
                    choose(GATES[i - 2])
                if i - 3 in GATES:
                    place(GATES[i - 3])

            stats_x2(NB - 1)
            aggr_x2(NB - 1)
            eps_x2(NC - 1, NC)
            choose(NC - 2)
            place(NC - 2)
            scale_x2(n, NC - 1, NC)
            dve.wait_ge(nmr2_done, n + 1)
            for b in range(LAST + 1, NB, 2):
                dve.tensor_scalar(token_row[:, b, 0:D], token_row[:, b, D:2 * D], rstd2[:, b:b + 1], nmr2[:, b:b + 1],
                                  ALU.mult, ALU.add).then_inc(xn2_dve, 1)
            ev_gate(NC - 1)
            choose(NC - 1)
            dve.wait_ge(count_mm, 1)
            dve.tensor_tensor(steer[:, 2 * NBLK:], bankU[:, 0:NE], cf[:, C_REG:C_REG + NE], ALU.add).then_inc(pad_rows, 1)
            place(NC - 1)
            dve.wait_ge(fill_done, 2)
            step(dve.tensor_tensor(nbc, bankU[:, 0:NE].unsqueeze(2).to_broadcast([128, NE, NB]),
                                   cf[:, C_J:C_J + NE * NB].rearrange("p (e j) -> p e j", e=NE), ALU.is_gt))
            step(dve.tensor_reduce(nblk[:], nbc, axis=AX.X, op=ALU.add))
            step(dve.tensor_tensor_scan(bend[:], ones8[:], nblk[:], 0.0, ALU.mult, ALU.add))
            step(dve.tensor_tensor(ble, bend[:].unsqueeze(1).to_broadcast([128, NBLK, NE]),
                                   cf[:, C_B:C_B + NBLK * NE].rearrange("p (n e) -> p n e", n=NBLK), ALU.is_le))
            step(dve.tensor_tensor(bgone, ble, nblk[:].unsqueeze(1).to_broadcast([128, NBLK, NE]), ALU.mult))
            step(dve.tensor_reduce(bexpf[:], ble, axis=AX.X, op=ALU.add))
            step(dve.tensor_reduce(bgonef[:], bgone, axis=AX.X, op=ALU.add))
            step(dve.scalar_tensor_tensor(bwithin[:], bgonef[:], -128.0, cf[:, C_B128:C_B128 + NBLK], ALU.mult, ALU.add))
            step(dve.scalar_tensor_tensor(browf[:], bexpf[:], float(REGION), bwithin[:], ALU.mult, ALU.add))
            dve.tensor_scalar(steer[:, 0:NBLK], bexpf[:], float(NE - 1), None, ALU.min).then_inc(block_rows, 1)
            dve.tensor_scalar(steer[:, NBLK:2 * NBLK], browf[:], float(NE * REGION), None, ALU.min).then_inc(block_rows, 1)

            def relu(k):
                dve.wait_ge(h_mm, 2 * k + 2)
                dve.wait_ge(w_in[k % WBUF], 16 * (k // WBUF + 1))
                if k >= 2:
                    dve.wait_ge(y_mm, k - 1)
                for c in range(2, 4):
                    dve.tensor_scalar(hT[:, k % 2, c, :], bankC_[2 * (k % 2) + 1][:, (c - 2) * 128:(c - 1) * 128],
                                      wblk[:, k % WBUF, W_B1 + c:W_B1 + c + 1], 0.0, ALU.add, ALU.max).then_inc(h_dve, 1)

            def finish(k):
                dve.wait_ge(y_mm, k + 1)
                dve.wait_ge(res_done, k + 1)
                if k >= OBUF:
                    dve.wait_ge(out_sent[k % OBUF], 16 * (k // OBUF))
                dve.scalar_tensor_tensor(outb[:, k % OBUF, :], [bankU, bankX][k % 2][:, 0:D], tg[:, 1:2], res[:, k % 2, :],
                                         ALU.mult, ALU.add).then_inc(out_done, 1)

            for k in range(NBLK):
                relu(k)
                if k >= 1:
                    finish(k - 1)
            finish(NBLK - 1)

        @block.tensor
        def _(pe):
            pe.wait_ge(ld_const, 16)
            for c in range(NC):
                pe.wait_ge(ld_ctx[c], 16)
                if c >= 2:
                    pe.wait_ge(k_lo, c - 1)
                pe.matmul(kbank[c % 2], w_sb[:, 1, :], ctx_sb[:, TOKS[c]], start=True, stop=True).then_inc(k_mm, 1)
                pe.wait_ge(xn_done, CB * (c + 1))
                if c >= 2:
                    pe.wait_ge(xnT_ev, c - 1)
                for j in range(CB):
                    ins = pe.transpose(xbank[c % 2][:, j * T:(j + 1) * T], xn[:, c % 2, j, :], ident)
                ins.then_inc(xnT_mm, 1)
                if c >= 2:
                    pe.wait_ge(v_32, c - 1)
                for j in range(CB):
                    b = c * CB + j
                    ins = pe.matmul(vbank[c % 2][:, j * D:(j + 1) * D], ctx_sb[:, b * T:(b + 1) * T], w_sb[:, 2, :],
                                    start=True, stop=True)
                ins.then_inc(v_mm, 1)
                pe.wait_ge(xnT_ev, c + 1)
                if c >= 2:
                    pe.wait_ge(q_lo, c - 1)
                pe.matmul(qbank[c % 2][:], w_sb[:, 0, :], xnT[:, c % 2, :], start=True, stop=True).then_inc(q_mm, 1)

            def scores(b, g):
                if b or g >= 2:
                    pe.wait_ge(max_done, 4 * b + g - 1)
                else:
                    pe.wait_ge(xnT_ev, NC)
                if g == 0:
                    pe.wait_ge(k_ready[b // CB], 16)
                    pe.wait_ge(q_ready[b // CB], 64)
                for i in range(4):
                    ins = pe.matmul(bankA[g % 2][:, i * T:(i + 1) * T], q_st[:, g, i, b * T:(b + 1) * T],
                                    k_st[:, g, b * T:(b + 1) * T], start=True, stop=True)
                ins.then_inc(s1_mm, 1)

            def shifted(b, g):
                if g == 0:
                    pe.wait_ge(m_ready[b % 4], 64 * (b // 4 + 1))
                if b >= 1 and g % 2 == 0:
                    pe.wait_ge(exp_done, 2 * b - 1 + g // 2)
                if b == 0 and g == 0:
                    pe.wait_ge(v_32, NC)
                    pe.wait_ge(k_lo, NC)
                    pe.wait_ge(v_lo, NC)
                    pe.wait_ge(v_hi, NC)
                pe.matmul(bankC_[g].rearrange("p (i t) -> p i t", i=4), k_st[:, g, b * T:(b + 1) * T],
                          q_st[:, g, :, b * T:(b + 1) * T], start=True, stop=True).then_inc(s2_mm, 1)

            def times_v(b, g):
                if g == 0:
                    pe.wait_ge(usum_done, b) if b else pe.wait_ge(q_lo, NC)
                if g % 2 == 0:
                    pe.wait_ge(exp_done, 2 * b + 1 + g // 2)
                    pe.wait_ge(lo_pool, 2 * b + 1 + g // 2)
                if g == 3:
                    pe.wait_ge(lo_dve, b + 1)
                for h in range(4 * g, 4 * g + 4):
                    u = bankU[:, h * VC:(h + 1) * VC]
                    s = slice(h * T, (h + 1) * T)
                    pe.matmul(u, hi_of(prob[:, b % 2, s]), v_sb[:, b, h, :], start=True, stop=False)
                    ins = pe.matmul(u, prob_lo[:, b % 2, s], v_sb[:, b, h, :], start=False, stop=True)
                ins.then_inc(pv_mm, 1)


            def bank_x_free(i):
                for read, n in ((x2T_ev, ended(i, 0)), (gate_ev, ended(i, 1)), (base_done, ended(i, 3))):
                    if n:
                        pe.wait_ge(read, n)

            def max_T(b):
                i = b + 1
                pe.wait_ge(m_lo, b + 1)
                pe.wait_ge(ld_half, 16)
                if b == 0:
                    pe.wait_ge(q_lo, NC)
                if i > OUT_LAG:
                    pe.wait_ge(x2_done, i - OUT_LAG)
                elif b:
                    pe.wait_ge(mT_ev, b)
                bank_x_free(i)
                for g in range(NG):
                    ins = pe.transpose(bankX[0:8, g * T // 2:(g + 1) * T // 2].bitcast(F16),
                                       mcol[:, b % 2, 8 * g:8 * g + 8], ident_h)
                ins.then_inc(mT_mm, 1)

            def attn_T(b):
                i = b + OUT_LAG
                pe.wait_ge(attn_done, b + 1)
                pe.wait_ge(mT_ev, min(NB, i))
                if b:
                    pe.wait_ge(x2_done, b)
                bank_x_free(i)
                pe.transpose(bankX[:, 0:T], attn[:, b % 2, :], ident).then_inc(attnT_mm, 1)

            def times_wo(b):
                pe.wait_ge(attnT_ev, b + 1)
                pe.matmul(bankX[:, 128:256], attnT[:, b % 2, :], w_sb[:, 3, :], start=True, stop=True).then_inc(wo_mm, 1)

            def x2_T(c, x2s):
                pe.wait_ge(x2_done, x2s)
                if c:
                    pe.wait_ge(gate_ev, c)
                for j in range(CB):
                    b = c * CB + j
                    pe.wait_ge(xn2_act, of_act(b))
                    if of_dve(b):
                        pe.wait_ge(xn2_dve, of_dve(b))
                    ins = pe.transpose(bankX[:, j * T:(j + 1) * T], token_row[:, b, 0:D], ident)
                ins.then_inc(x2T_mm, 1)

            def gate(c, x2s):
                pe.wait_ge(x2_done, x2s)
                pe.wait_ge(x2T_ev, c + 1)
                for j in range(CB):
                    ins = pe.matmul(bankX[:, j * NE:(j + 1) * NE], x2T[:, j * T:(j + 1) * T], gate_sb, start=True, stop=True)
                ins.then_inc(gate_mm, 1)

            def rank(c, x2s):
                pe.wait_ge(onehot_done, c + 1)
                pe.wait_ge(x2_done, x2s)
                own = onehot_h[:, c * CB:(c + 1) * CB, :].rearrange("p b e -> p (b e)")
                pe.matmul(bankX[:, 0:CB * NE], before_h, own, start=True, stop=False)
                for j in range(c * CB):
                    pe.matmul(bankX[:, 0:CB * NE], ones_h, onehot_h[:, j, :].unsqueeze(1).to_broadcast([128, CB, NE]),
                              start=False, stop=False)
                for j in range(1, CB):
                    ins = pe.matmul(bankX[:, j * NE:CB * NE], ones_h, own[:, 0:(CB - j) * NE], start=False, stop=(j == CB - 1))
                ins.then_inc(rank_mm, 1)

            for i in range(ROUNDS):
                now, s2_b, pv_b, out_b = i < NB, i - S2_LAG, i - PV_LAG, i - OUT_LAG
                shift, use_v, out_now = 0 <= s2_b < NB, 0 <= pv_b < NB, 0 <= out_b < NB
                if now:
                    scores(i, 0)
                if shift:
                    shifted(s2_b, 0)
                if now:
                    scores(i, 1)
                if 0 <= i - 1 < NB:
                    max_T(i - 1)
                if shift:
                    shifted(s2_b, 1)
                if use_v:
                    times_v(pv_b, 0)
                if now:
                    scores(i, 2)
                if shift:
                    shifted(s2_b, 2)
                if use_v:
                    times_v(pv_b, 1)
                if out_now:
                    attn_T(out_b)
                if now:
                    scores(i, 3)
                if use_v:
                    times_v(pv_b, 2)
                if out_now:
                    times_wo(out_b)
                if shift:
                    shifted(s2_b, 3)
                if use_v:
                    times_v(pv_b, 3)
                x2s = i - OUT_LAG + 1
                if i - 1 in GATES:
                    gate(GATES[i - 1], x2s)
                if i - 3 in GATES:
                    rank(GATES[i - 3], x2s)
                if i in GATES:
                    if ended(i + 1, 3):
                        pe.wait_ge(base_done, ended(i + 1, 3))
                    x2_T(GATES[i], x2s)
            rank(NC - 2, NB)
            pe.wait_ge(base_done, NC - 1)
            x2_T(NC - 1, NB)
            gate(NC - 1, NB)
            pe.wait_ge(onehot_done, NC)
            pe.wait_ge(usum_done, NB)
            for b in range(NB):
                ins = pe.matmul(bankU[:, 0:NE], ones_h, onehot_h[:, b, :], start=(b == 0), stop=(b == NB - 1))
            ins.then_inc(count_mm, 1)
            pe.wait_ge(gate_ev, NC)
            rank(NC - 1, NB)

            def block_T(k):
                pe.wait_ge(blk_in[k % NBUF], 16 * (k // NBUF + 1))
                if k >= 2:
                    pe.wait_ge(bT_ev, k - 1)
                else:
                    pe.wait_ge(max_done, 4 * NB)
                pe.transpose(bankA[k % 2][:, 0:128], blk[:, k % NBUF, 0:D], ident).then_inc(bT_mm, 1)

            def hidden(k):
                pe.wait_ge(bT_ev, k + 1)
                pe.wait_ge(w_in[k % WBUF], 16 * (k // WBUF + 1))
                if k >= 2:
                    pe.wait_ge(h_act, 2 * (k - 1))
                    pe.wait_ge(h_dve, 2 * (k - 1))
                else:
                    pe.wait_ge(exp_done, 2 * NB)
                for half in range(2):
                    for c in range(2):
                        ins = pe.matmul(bankC_[2 * (k % 2) + half][:, c * 128:(c + 1) * 128],
                                        wblk[:, k % WBUF, (2 * half + c) * 128:(2 * half + c + 1) * 128], bT[:, k % 2, :],
                                        start=True, stop=True)
                    ins.then_inc(h_mm, 1)

            def down(k):
                pe.wait_ge(h_act, 2 * (k + 1))
                pe.wait_ge(h_dve, 2 * (k + 1))
                if k >= 2:
                    pe.wait_ge(out_done, k - 1)
                else:
                    pe.wait_ge(block_rows, 2)
                for c in range(HC):
                    ins = pe.matmul([bankU, bankX][k % 2][:, 0:D], hT[:, k % 2, c, :],
                                    wblk[:, k % WBUF, W_W2 + c * D:W_W2 + (c + 1) * D], start=(c == 0), stop=(c == HC - 1))
                ins.then_inc(y_mm, 1)

            block_T(0)
            for k in range(NBLK):
                if k + 1 < NBLK:
                    block_T(k + 1)
                hidden(k)
                if k >= 1:
                    down(k - 1)
            down(NBLK - 1)


def kernel(x, ctx_1024, g_xattn, g_ffn, L0_xattn_wq_w, L0_xattn_wq_b, L0_xattn_wk_w, L0_xattn_wk_b, L0_xattn_wv_w,
           L0_xattn_wv_b, L0_xattn_wo_w, L0_xattn_wo_b, L0_ffn_gate_w, L0_ffn_gate_b, L0_ffn_w1, L0_ffn_b1, L0_ffn_w2,
           L0_ffn_b2):
    import numpy as np
    import concourse.bacc as bacc
    from concourse.bass_utils import run_bass_kernel_spmd

    a = {n: np.asarray(v) for n, v in dict(
        x=x, ctx=ctx_1024, gx=g_xattn, gf=g_ffn, wq=L0_xattn_wq_w, wk=L0_xattn_wk_w, wv=L0_xattn_wv_w, wo=L0_xattn_wo_w,
        bq=L0_xattn_wq_b, bk=L0_xattn_wk_b, bv=L0_xattn_wv_b, bo=L0_xattn_wo_b, gw=L0_ffn_gate_w, gb=L0_ffn_gate_b,
        w1=L0_ffn_w1, b1=L0_ffn_b1, w2=L0_ffn_w2, b2=L0_ffn_b2).items()}
    p = np.arange(128)
    constf = np.zeros((128, NCONST), np.float32)
    constf[:, C_ID:C_ID + 128] = np.eye(128)
    constf[:, C_W:C_GATE] = np.concatenate([a[n].T for n in ("wq", "wk", "wv", "wo")], 1)
    constf[:, C_GATE:C_COL] = a["gw"].T
    constf[:, C_COL] = a["bq"]
    constf[:, C_COL + 1] = a["bk"]
    constf[:, C_J:C_J + NE * NB] = np.tile(128.0 * np.arange(NB), NE)
    constf[:, C_E:C_E + NE] = NE - np.arange(NE)
    constf[:, C_B:C_B + NBLK * NE] = np.repeat(np.arange(NBLK), NE)
    constf[:, C_B128:C_B128 + NBLK] = 128 * np.arange(NBLK)
    constf[:, C_REG:C_REG + NE] = REGION * np.arange(NE)
    constf[:, C_TOK:C_TOK + NB] = 128 * np.arange(NB)[None, :] + p[:, None]
    consth = np.concatenate([np.eye(128), p[:, None] < p[None, :], np.ones((128, 128))], 1).astype(np.float16)
    ins = {
        "x": a["x"],
        "ctxT": a["ctx"].transpose(2, 0, 1).reshape(D, NTOK),
        "vecs": np.concatenate([a[n] for n in ("bv", "bo", "gb", "gx", "gf")]),
        "wexp": np.concatenate([
            a["w1"].transpose(0, 2, 1),
            a["w2"].transpose(0, 2, 1).reshape(NE, HC, 128, D).transpose(0, 2, 1, 3).reshape(NE, 128, HC * D),
            a["b1"].reshape(NE, HC, 128).transpose(0, 2, 1)], 2),
        "b2r": a["b2"],
        "constf": constf,
        "consth": consth,
        "onesh": np.ones((NG, 4, DH, NTOK), np.float16),
    }
    ins = {n: np.ascontiguousarray(v) for n, v in ins.items()}
    nc = bacc.Bacc("TRN2", target_bir_lowering=False, num_devices=1)
    aps = {n: nc.dram_tensor("in_" + n, v.shape, mybir.dt.from_np(v.dtype), kind="ExternalInput").ap() for n, v in ins.items()}
    out = nc.dram_tensor("out", (NTOK, D), F32, kind="ExternalOutput").ap()
    program(nc, **aps, out=out)
    r = run_bass_kernel_spmd(nc, [{"in_" + n: v for n, v in ins.items()}], core_ids=[0])
    return r.results[0]["out"].reshape(NB, T, D)
```

```python
import concourse.bass as bass
from concourse import mybir
from contextlib import ExitStack

F32 = mybir.dt.float32
F16 = mybir.dt.float16
BF16 = mybir.dt.bfloat16
I32 = mybir.dt.int32
U32 = mybir.dt.uint32
ALU = mybir.AluOpType
ACT = mybir.ActivationFunctionType
AX = mybir.AxisListType

NB, T, D = 16, 128, 128
NTOK = NB * T
NH, DH = 16, 8
NG = 4
SLOT = 32
NE, HID = 8, 512
HC = HID // 128
NBLK = NTOK // 128 + NE - 1
CB = 4
NC = NB // CB
SURE = NB + NE // 2
CT = CB * T
EPS = 1e-5
SCALE = float(DH) ** -0.5
VC = 2 * (DH + 1)
ROW = 2 * D + 8
W_B1, W_B2 = HID, HID + HC
WCOPY = W_B2 + D
WCOL = WCOPY + HC * D

REGION = 2 * NTOK
SPARE = (NE - 1) * REGION + NTOK + 128
NROWS = NE * REGION

C_ID = 0
C_W = C_ID + 128
C_GATE = C_W + 4 * D
C_COL = C_GATE + NE
C_J = C_COL + 3
C_E = C_J + NE * NB
C_B = C_E + NE
C_B128 = C_B + NBLK * NE
C_REG = C_B128 + NBLK
C_TOK = C_REG + NE
NCONST = C_TOK + NB
V_BO, V_GB, V_GAIN = 0, D, D + NE
NVEC = V_GAIN + 2
BUSY_AT_START, BUSY_BEFORE_ROWS, BUSY_BEFORE_BLOCKS = 14, 20, 30


def program(nc, x, ctxT, vecs, wexp, b2r, constf, consth, onesh, out):
    ctx = ExitStack()
    with ctx:
        def sb(name, shape, dt=F32):
            return ctx.enter_context(nc.sbuf_tensor(name, shape, dt))

        def ps(name, shape, dt=F32):
            return ctx.enter_context(nc.psum_tensor(name, shape, dt))

        def sem(name):
            return ctx.enter_context(nc.semaphore(name))

        q_dram = nc.dram_tensor("q_stack", (NG, 4, DH, 3, NTOK), F16).ap()
        k_dram = nc.dram_tensor("k_stack", (NG, 4, SLOT, NTOK), F16).ap()
        sorted_dram = nc.dram_tensor("sorted_rows", (NROWS, ROW), F32).ap()

        x_sb = sb("x_sb", [128, NB, D])
        ctx_sb = sb("ctx_sb", [128, NTOK])
        vec_sb = sb("vec_sb", [128, NVEC])
        tg = sb("tg", [128, 2])
        cf = sb("cf", [128, NCONST])
        ch = sb("ch", [128, 3 * 128], F16)
        experts = sb("experts", [128, NE, WCOL])
        ident = cf[:, C_ID:C_ID + 128]
        w_sb = cf[:, C_W:C_GATE].rearrange("p (n d) -> p n d", n=4)
        gate_sb = cf[:, C_GATE:C_GATE + NE]
        cols_sb = cf[:, C_COL:C_J]
        ident_h = ch[:, 0:128]
        before_h = ch[:, 128:256]
        ones_h = ch[:, 256:384]

        stats = sb("stats", [128, NB, 6])
        mv = sb("mv", [128, NB, 2])
        rstd = sb("rstd", [128, NB])
        std = sb("std", [128, NB])
        eps_col = sb("eps_col", [128, 1])
        nmr = sb("nmr", [128, NB])
        q_part = sb("q_part", [128, 2, 2, CT], F16)
        k_part = sb("k_part", [128, 2, 2, CT], F16)
        v_sb = sb("v_sb", [128, NB, NH, VC], F16)
        q_st = sb("q_st", [128, NG, 4, NTOK], F16)
        k_st = sb("k_st", [128, NG, NTOK], F16)
        ones_row = sb("ones_row", [1, 128])
        gbias = sb("gbias", [128, D])

        mx = sb("mx", [128, 2, NH])
        mcol = sb("mcol", [128, 2, 32], F16)
        mT = sb("mT", [8, 2, NG, T], F16)
        prob = sb("prob", [128, 2, NH * T])
        xn = prob[:, 0, 0:2 * CT].rearrange("p (n b d) -> p n b d", n=2, b=CB)
        xnT = prob[:, 0, 2 * CT:4 * CT].rearrange("p (n t) -> p n t", n=2)
        prob_lo = sb("prob_lo", [128, 2, NH * T], F16)
        usum = sb("usum", [128, NH, DH + 1])
        rden = sb("rden", [128, NH])
        attn = sb("attn", [128, 2, D])
        attnT = sb("attnT", [128, 2, T])
        token_row = sb("token_row", [128, NB, ROW])
        stats2 = sb("stats2", [128, NB, 6])
        mv2 = sb("mv2", [128, NB, 2])
        std2 = sb("std2", [128, NB])
        rstd2 = sb("rstd2", [128, NB])
        nmr2 = sb("nmr2", [128, NB])
        x2T = ctx_sb[:, 0:CT]
        logit = sb("logit", [128, NB, NE])

        lmax = sb("lmax", [128, NB])
        isbest = sb("isbest", [128, NB, NE])
        picked = sb("picked", [128, NB, NE])
        wgt = sb("wgt", [128, NB, NE])
        onehot_h = sb("onehot_h", [128, NB, NE], F16)
        base = sb("base", [128, NB, NE])
        wmax = sb("wmax", [128, NB])
        ones8 = sb("ones8", [128, NE])
        nbc = ctx_sb[:, CT:CT + NE * NB].rearrange("p (e j) -> p e j", e=NE)
        ble, bgone = (ctx_sb[:, n * CT:n * CT + NBLK * NE].rearrange("p (n e) -> p n e", n=NBLK) for n in (2, 3))
        nblk = sb("nblk", [128, NE])
        bend = sb("bend", [128, NE])
        slotf = sb("slotf", [128, NB])
        slot = sb("slot", [128, NB], U32)
        bexpf = sb("bexpf", [128, NBLK])
        bgonef = sb("bgonef", [128, NBLK])
        bwithin = sb("bwithin", [128, NBLK])
        browf = sb("browf", [128, NBLK])
        steer = sb("steer", [128, NBLK + NE + NBLK], I32)
        fill = sb("fill", [128, ROW])
        NBUF, WBUF, OBUF = 8, 6, 4
        q_words = q_st[:].rearrange("p g i t -> p (g i t)").bitcast(F32)
        taken = [0]

        def over_q(*shape):
            size = 1
            for n in shape:
                size *= n
            at, taken[0] = taken[0], taken[0] + size
            names = "abc"[:len(shape)]
            return q_words[:, at:at + size].rearrange(f"p ({' '.join(names)}) -> p {' '.join(names)}",
                                                      **dict(zip(names, shape)))

        blk = over_q(NBUF, ROW)
        wblk = over_q(WBUF, WCOPY)
        bT = over_q(2, 128)
        hT = over_q(2, HC, 128)
        res = over_q(2, D)
        outb = over_q(OBUF, D)

        bankA = [ps(f"bankA{n}", [128, 512]) for n in range(2)]
        bankC = ps("bankC", [128, 4 * 512])
        bankU = ps("bankU", [128, 512])
        bankX = ps("bankX", [128, 512])
        bankC_ = [bankC[:, 512 * i:512 * i + 512] for i in range(4)]

        ld_const, ld_half, ld_vec, ld_exp, ld_b2 = (sem(n) for n in ("ld_const", "ld_half", "ld_vec", "ld_exp", "ld_b2"))
        ld_x = [sem(f"ld_x{c}") for c in range(NC)]
        ld_ctx = [sem(f"ld_ctx{c}") for c in range(NC)]
        attn_zero = sem("attn_zero")
        q_zero = [sem(f"q_zero{c}") for c in range(NC)]
        ones_in_k, v_init, fill_done, ids_done = (sem(n) for n in ("ones_in_k", "v_init", "fill_done", "ids_done"))
        eps_set, bn1, agg1, std1, rst1, nmr1, xn_dve, xn_pool = (
            sem(n) for n in ("eps_set", "bn1", "agg1", "std1", "rst1", "nmr1", "xn_dve", "xn_pool"))
        xnT_mm, xnT_ev, q_mm, k_mm, v_mm = (sem(n) for n in ("xnT_mm", "xnT_ev", "q_mm", "k_mm", "v_mm"))
        q_hi, q_lo, k_hi, k_lo, v_hi, v_lo = (
            sem(n) for n in ("q_hi", "q_lo", "k_hi", "k_lo", "v_hi", "v_lo"))
        q_written = [sem(f"q_written{c}") for c in range(NC)]
        k_written = [sem(f"k_written{c}") for c in range(NC)]
        q_ready = [sem(f"q_ready{c}") for c in range(NC)]
        k_ready = [sem(f"k_ready{c}") for c in range(NC)]
        tg_done, b2g_done, bias_mm, gbias_done, xb_done = (
            sem(n) for n in ("tg_done", "b2g_done", "bias_mm", "gbias_done", "xb_done"))

        s1_mm, max_done, m_hi, m_lo, mT_mm, mT_ev = (
            sem(n) for n in ("s1_mm", "max_done", "m_hi", "m_lo", "mT_mm", "mT_ev"))
        m_ready = [sem(f"m_ready{n}") for n in range(4)]
        s2_mm, exp_done, lo_pool, lo_dve, pv_mm = (
            sem(n) for n in ("s2_mm", "exp_done", "lo_pool", "lo_dve", "pv_mm"))
        usum_done, rden_done, attn_done, attnT_mm, attnT_ev, wo_mm, x2_done = (
            sem(n) for n in ("usum_done", "rden_done", "attn_done", "attnT_mm", "attnT_ev", "wo_mm", "x2_done"))
        bn2, agg2, std2_done, rst2, nmr2_done, xn2_act, xn2_dve = (
            sem(n) for n in ("bn2", "agg2", "std2_done", "rst2", "nmr2_done", "xn2_act", "xn2_dve"))
        x2T_mm, x2T_ev, gate_mm, gate_ev = (sem(n) for n in ("x2T_mm", "x2T_ev", "gate_mm", "gate_ev"))
        route, onehot_done, rank_mm, base_done, slot_done, count_mm, pad_rows, block_rows = (
            sem(n) for n in ("route", "onehot_done", "rank_mm", "base_done", "slot_done", "count_mm", "pad_rows", "block_rows"))
        scattered, spare_init, padded = (sem(n) for n in ("scattered", "spare_init", "padded"))
        blk_in = [sem(f"blk_in{n}") for n in range(NBUF)]
        w_in = [sem(f"w_in{n}") for n in range(WBUF)]
        bT_mm, bT_ev, h_mm, h_act, h_dve, y_mm, res_done, out_done = (
            sem(n) for n in ("bT_mm", "bT_ev", "h_mm", "h_act", "h_dve", "y_mm", "res_done", "out_done"))
        out_sent = [sem(f"out_sent{n}") for n in range(OBUF)]

        TOKS = [slice(c * CT, (c + 1) * CT) for c in range(NC)]

        xbank, kbank, vbank, qbank = bankU, *bankC_[0:3]

        S2_LAG = 3
        PV_LAG = 4
        OUT_LAG = 5
        DRAIN = NB - PV_LAG
        NORM2_ROUND = 13


        def lo_heads(b):
            return 14 if b < DRAIN else 8

        def lo_count(b, n):
            return 2 * b + n + 1 if b < DRAIN else DRAIN + b + 1

        LAST = NB - CB

        def of_act(b):
            return b + 1 if b < LAST else LAST + (b - LAST) // 2 + 1

        def of_dve(b):
            return 0 if b < LAST else (b - LAST + 1) // 2

        def max_bank(b):
            return bankX if b < NB - 1 else bankA[0]

        def hi_of(p):
            return p.bitcast(BF16).rearrange("p (n two) -> p n two", two=2)[:, :, 1]

        block = ctx.enter_context(nc.Block())

        def first_rows(engine, at, count, max_row=SPARE):
            return nc.values_load_multi_w_load_instructions(steer[0:1, at:at + count], engines=(engine,),
                                                            min_val=0, max_val=max_row)[1]

        def more_blocks(engine, kind):
            return engine.If(first_rows(kind, SURE, 1)[0] < SPARE)

        def pad_regions(queue, engine, e0, e1):
            queue.wait_ge(pad_rows, 1)
            queue.wait_ge(fill_done, 1)
            for row in first_rows(engine, NBLK + e0, e1 - e0):
                queue.dma_start(sorted_dram[bass.ds(row, 128), :], fill[:]).then_inc(padded, 16)

        @block.sync
        def _(sp):
            def load_x(c):
                sp.dma_start(x_sb[:, c * CB:(c + 1) * CB, :],
                             x[c * CB:(c + 1) * CB].rearrange("b t d -> t b d")).then_inc(ld_x[c], 16)

            def load_ctx(c):
                sp.dma_start(ctx_sb[:, TOKS[c]], ctxT[:, TOKS[c]]).then_inc(ld_ctx[c], 16)

            load_x(0)
            sp.dma_start(cf[:], constf).then_inc(ld_const, 16)
            load_ctx(0)
            load_x(1)
            sp.dma_start(vec_sb[:], vecs.partition_broadcast(128)).then_inc(ld_vec, 16)
            load_ctx(1)
            load_x(2)
            load_x(3)
            for g in range(NG):
                sp.dma_start(k_dram[g, :, 3 * DH:SLOT], onesh[g]).then_inc(ones_in_k, 16)

            def write_k(c):
                for n, part, made in ((0, 0, k_hi), (2, 0, k_hi), (1, 1, k_lo)):
                    sp.wait_ge(made, c + 1)
                    sp.dma_start(k_dram[:, :, n:3 * DH:3, TOKS[c]].rearrange("g i d t -> (g i) d t"),
                                 k_part[:, c % 2, part, :]).then_inc(k_written[c], 16)

            def write_q(c):
                q_rows = q_dram[:, :, :, :, TOKS[c]].rearrange("g i d n t -> (g i d) n t")
                sp.wait_ge(q_hi, c + 1)
                sp.dma_start(q_rows[:, 0], q_part[:, c % 2, 0, :]).then_inc(q_written[c], 16)
                sp.wait_ge(q_lo, c + 1)
                sp.dma_start(q_rows[:, 1:3], q_part[:, c % 2]).then_inc(q_written[c], 16)

            def read_k(c):
                sp.wait_ge(ones_in_k, 16 * NG)
                sp.wait_ge(k_written[c], 48)
                sp.dma_start(k_st[:, :, TOKS[c]],
                             k_dram[:, :, :, TOKS[c]].rearrange("g i r t -> (i r) g t")).then_inc(k_ready[c], 16)

            def read_q(c):
                sp.wait_ge(q_zero[c], NG)
                sp.wait_ge(q_written[c], 32)
                for i in range(4):
                    sp.dma_start(q_st[SLOT * i:SLOT * i + 3 * DH, :, i, TOKS[c]],
                                 q_dram[:, i, :, :, TOKS[c]].rearrange("g d n t -> (d n) g t")).then_inc(q_ready[c], 16)

            def send_max(b):
                sp.wait_ge(mT_ev, b + 1)
                if b >= 4:
                    sp.wait_ge(m_ready[b % 4], 64 * (b // 4))
                for i in range(4):
                    sp.dma_start(q_st[SLOT * i + 3 * DH:SLOT * i + 3 * DH + 2, :, i, b * T:(b + 1) * T],
                                 mT[2 * i:2 * i + 2, b % 2]).then_inc(m_ready[b % 4], 16)

            for c in range(2):
                write_k(c)
                write_q(c)
                read_k(c)
                read_q(c)
                if c == 0:
                    sp.dma_start(ch[:], consth).then_inc(ld_half, 16)
                    load_ctx(2)
                    load_ctx(3)
            for b in range(NB):
                send_max(b)
                c = 2 + b // 4
                if b >= NB - NE:
                    e = b - (NB - NE)
                    sp.dma_start(experts[:, e, 0:W_B2], wexp[e, :, 0:W_B2]).then_inc(ld_exp, 16)
                    sp.dma_start(experts[:, e, WCOPY:WCOL], wexp[e, :, W_B2:]).then_inc(ld_exp, 16)
                elif b % 4 == 0:
                    write_k(c)
                elif b % 4 == 1:
                    write_q(c)
                elif b % 4 == 2:
                    read_k(c)
                else:
                    read_q(c)
            sp.dma_start(experts[:, :, W_B2:WCOPY], b2r.partition_broadcast(128)).then_inc(ld_b2, 16)
            sp.wait_ge(fill_done, 1)
            sp.dma_start(sorted_dram[SPARE:SPARE + 128, :], fill[:]).then_inc(spare_init, 16)

            pad_regions(sp, mybir.EngineType.SP, 0, NE // 2)

            sp.wait_ge(ld_exp, 32 * NE)
            sp.wait_ge(b2g_done, 1)
            sp.wait_ge(block_rows, 2)

            def load_block(k, row):
                if k >= NBUF:
                    sp.wait_ge(bT_mm, k - NBUF + 1)
                    sp.wait_ge(out_sent[(k - NBUF) % OBUF], 16 * ((k - NBUF) // OBUF + 1))
                sp.dma_start(blk[:, k % NBUF, :], sorted_dram[bass.ds(row, 128), :]).then_inc(blk_in[k % NBUF], 16)

            def load_weights(k, row):
                if k >= WBUF:
                    sp.wait_ge(y_mm, k - WBUF + 1)
                    sp.wait_ge(res_done, k - WBUF + 1)
                sp.dma_start(wblk[:, k % WBUF, :], experts[:, bass.ds(row // REGION, 1), 0:WCOPY]).then_inc(w_in[k % WBUF], 16)

            AT_ONCE, AHEAD = SURE // 4, 1

            def load_blocks(k0, k1):
                rows = dict(zip(range(k0, k1), first_rows(mybir.EngineType.SP, k0, k1 - k0)))
                if k0 == 0:
                    for k in range(AHEAD):
                        load_weights(k, rows[k])
                    sp.wait_ge(spare_init, 16)
                    sp.wait_ge(padded, 16 * NE)
                    sp.wait_ge(scattered, 16 * NB)
                for k in range(k0, k1):
                    load_block(k, rows[k])
                    if k >= AHEAD:
                        load_weights(k, rows[k])

            for k0 in range(0, SURE, AT_ONCE):
                load_blocks(k0, k0 + AT_ONCE)
            with more_blocks(sp, mybir.EngineType.SP):
                load_blocks(SURE, NBLK)

        @block.gpsimd
        def _(pool):
            pool.memset(q_st[:, NG - 1, :, TOKS[0]].bitcast(U32), 0).then_inc(q_zero[0], 1)
            pool.memset(v_sb[:, :, :, DH:DH + 1], 1.0).then_inc(v_init, 1)
            pool.memset(v_sb[:, :, :, VC - 1:VC], 0.0).then_inc(v_init, 1)
            pool.memset(fill[:], 1.0).then_inc(fill_done, 1)
            pool.memset(ones8[:], 1.0).then_inc(fill_done, 1)
            pool.memset(ones_row[:], 1.0).then_inc(fill_done, 1)

            def zero_q(c):
                for g in range(NG):
                    pool.memset(q_st[:, g, :, TOKS[c]].bitcast(U32), 0).then_inc(q_zero[c], 1)

            def norm1(c):
                pool.wait_ge(nmr1, c + 1)
                if c >= 2:
                    pool.wait_ge(xnT_mm, c - 1)
                for b in range(c * CB, (c + 1) * CB):
                    pool.tensor_scalar(xn[:, c % 2, b % CB, :], x_sb[:, b, :], rstd[:, b:b + 1], nmr[:, b:b + 1],
                                       ALU.mult, ALU.add).then_inc(xn_pool, 1)

            norm1(1)
            zero_q(1)
            norm1(2)
            norm1(3)
            zero_q(2)
            zero_q(3)
            pool.wait_ge(gbias_done, 1)
            pool.wait_ge(xn_dve, CB)
            pool.wait_ge(xn_pool, NB - CB)
            for c in range(NC):
                pool.tensor_tensor(x_sb[:, c * CB:(c + 1) * CB, :], x_sb[:, c * CB:(c + 1) * CB, :],
                                   gbias[:].unsqueeze(1).to_broadcast([128, CB, D]), ALU.add).then_inc(xb_done, 1)

            def lo_part(b, n):
                h0, h1 = ((0, 8), (8, lo_heads(b)))[n]
                pool.wait_ge(exp_done, 2 * b + n + 1)
                if b >= 2:
                    pool.wait_ge(pv_mm, 4 * (b - 1))
                pool.tensor_tensor(prob_lo[:, b % 2, h0 * T:h1 * T], prob[:, b % 2, h0 * T:h1 * T],
                                   hi_of(prob[:, b % 2, h0 * T:h1 * T]), ALU.subtract).then_inc(lo_pool, 1)

            for b in range(NB):
                lo_part(b, 0)
                if b < DRAIN:
                    lo_part(b, 1)
            pool.wait_ge(ld_b2, 16)
            pool.wait_ge(tg_done, 1)
            pool.tensor_scalar(experts[:, :, W_B2:WCOPY], experts[:, :, W_B2:WCOPY],
                               tg[:, 1:2], 0.0, ALU.mult, ALU.add).then_inc(b2g_done, 1)
            pool.wait_ge(ids_done, 1)
            for b in range(NB):
                pool.wait_ge(slot_done, b // CB + 1)
                pool.wait_ge(xn2_act, of_act(b))
                if of_dve(b):
                    pool.wait_ge(xn2_dve, of_dve(b))
                pool.indirect_dma_start(sorted_dram, bass.IndirectOffsetOnAxis(ap=slot[:, b:b + 1], axis=0),
                                        token_row[:, b, :], None, bounds_check=NROWS - 1,
                                        oob_is_err=False).then_inc(scattered, 16)

            def residual_b2(k):
                pool.wait_ge(blk_in[k % NBUF], 16 * (k // NBUF + 1))
                pool.wait_ge(w_in[k % WBUF], 16 * (k // WBUF + 1))
                if k >= 2:
                    pool.wait_ge(out_done, k - 1)
                pool.tensor_tensor(res[:, k % 2, :], blk[:, k % NBUF, D:2 * D], wblk[:, k % WBUF, W_B2:WCOPY],
                                   ALU.add).then_inc(res_done, 1)

            def send(k):
                pool.wait_ge(out_done, k + 1)
                pool.indirect_dma_start(out, bass.IndirectOffsetOnAxis(ap=blk[:, k % NBUF, 2 * D:2 * D + 1].bitcast(U32), axis=0),
                                        outb[:, k % OBUF, :], None, bounds_check=NTOK - 1,
                                        oob_is_err=False).then_inc(out_sent[k % OBUF], 16)

            def blocks(k0, k1):
                for k in range(k0, k1):
                    residual_b2(k)
                    if k - 2 >= k0:
                        send(k - 2)
                send(k1 - 2)
                send(k1 - 1)

            def all_sent(n_blocks):
                for n in range(OBUF):
                    pool.wait_ge(out_sent[n], 16 * ((n_blocks - 1 - n) // OBUF + 1))

            blocks(0, SURE)
            pool.wait_ge(block_rows, 2)
            with more_blocks(pool, mybir.EngineType.Pool):
                blocks(SURE, NBLK)
                all_sent(NBLK)
            all_sent(SURE)

        @block.scalar
        def _(act):
            def std_x(c):
                act.wait_ge(agg1, CB * (c + 1))
                act.activation(std[:, c * CB:(c + 1) * CB], mv[:, c * CB:(c + 1) * CB, 1], ACT.Sqrt,
                               bias=eps_col[:]).then_inc(std1, 1)

            def k_hi_part(c):
                act.wait_ge(k_mm, c + 1)
                if c >= 2:
                    act.wait_ge(k_written[c - 2], 48)
                act.activation(k_part[:, c % 2, 0, :], kbank, ACT.Identity, bias=cols_sb[:, 1:2]).then_inc(k_hi, 1)

            def ev_xnT(c):
                act.wait_ge(xnT_mm, c + 1)
                if c >= 2:
                    act.wait_ge(q_mm, c - 1)
                act.activation(xnT[:, c % 2, :], xbank[:], ACT.Copy).then_inc(xnT_ev, 1)

            def v_hi_part(c):
                act.wait_ge(v_mm, c + 1)
                act.activation(v_sb[:, c * CB:(c + 1) * CB, :, 0:DH],
                               vbank.rearrange("p (b h d) -> p b h d", b=CB, h=NH), ACT.Copy).then_inc(v_hi, 1)

            def q_hi_part(c):
                act.wait_ge(q_mm, c + 1)
                if c >= 2:
                    act.wait_ge(q_written[c - 2], 32)
                act.activation(q_part[:, c % 2, 0, :], qbank, ACT.Identity, bias=cols_sb[:, 0:1]).then_inc(q_hi, 1)

            act.wait_ge(eps_set, 1)
            std_x(0)
            act.wait_ge(ld_const, 16)
            k_hi_part(0)
            std_x(1)
            ev_xnT(0)
            q_hi_part(0)
            std_x(2)
            act.wait_ge(v_init, 2)
            v_hi_part(0)
            std_x(3)
            k_hi_part(1)
            ev_xnT(1)
            q_hi_part(1)
            v_hi_part(1)
            act.wait_ge(ld_vec, 16)
            act.activation(tg[:], vec_sb[:, V_GAIN:V_GAIN + 2], ACT.Tanh).then_inc(tg_done, 1)
            act.wait_ge(bias_mm, 1)
            act.wait_ge(tg_done, 1)
            act.activation(gbias[:], bankX[:, 0:D], ACT.Copy, scale=tg[:, 0:1]).then_inc(gbias_done, 1)

            def exps(b, half):
                act.wait_ge(s2_mm, 4 * b + 2 * half + 2)
                if b >= 2:
                    act.wait_ge(pv_mm, 4 * (b - 1))
                s = slice(half * 1024, half * 1024 + 1024)
                act.activation(prob[:, b % 2, s], bankC[:, s], ACT.Exp, scale=SCALE).then_inc(exp_done, 1)

            def ev_mT(b):
                act.wait_ge(mT_mm, b + 1)
                if b >= 2:
                    act.wait_ge(m_ready[(b - 2) % 4], 64 * ((b - 2) // 4 + 1))
                act.activation(mT[:, b % 2].rearrange("p g t -> p (g t)"), max_bank(b)[0:8, 0:256].bitcast(F16), ACT.Copy).then_inc(mT_ev, 1)

            def ev_attnT(b):
                act.wait_ge(attnT_mm, b + 1)
                if b >= 2:
                    act.wait_ge(wo_mm, b - 1)
                act.activation(attnT[:, b % 2, :], bankX[:, 0:T], ACT.Copy).then_inc(attnT_ev, 1)

            def std_x2(c0, c1):
                act.wait_ge(agg2, c1 * CB)
                act.activation(std2[:, c0 * CB:c1 * CB], mv2[:, c0 * CB:c1 * CB, 1], ACT.Sqrt,
                               bias=eps_col[:]).then_inc(std2_done, 1)

            def norm2(n, batches):
                act.wait_ge(nmr2_done, n + 1)
                for b in batches:
                    act.activation(token_row[:, b, 0:D], token_row[:, b, D:2 * D], ACT.Identity,
                                   bias=nmr2[:, b:b + 1], scale=rstd2[:, b:b + 1]).then_inc(xn2_act, 1)

            def ev_x2T(c):
                act.wait_ge(x2T_mm, c + 1)
                if c >= 1:
                    act.wait_ge(gate_mm, c)
                act.activation(x2T, bankA[0][:], ACT.Copy).then_inc(x2T_ev, 1)

            for i in range(NB):
                if i < 2:
                    k_hi_part(i + 2)
                    v_hi_part(i + 2)
                    ev_xnT(i + 2)
                if i >= S2_LAG:
                    exps(i - S2_LAG, 0)
                if i >= 1:
                    ev_mT(i - 1)
                if i < 2:
                    q_hi_part(i + 2)
                if i >= OUT_LAG:
                    ev_attnT(i - OUT_LAG)
                if i >= S2_LAG:
                    exps(i - S2_LAG, 1)
                if i == NORM2_ROUND:
                    std_x2(0, 2)
                if i == NORM2_ROUND + 1:
                    norm2(0, range(4))
                if i == NORM2_ROUND + 2:
                    norm2(0, range(4, 6))

            ev_mT(NB - 1)
            exps(DRAIN + 1, 0)
            exps(DRAIN + 1, 1)
            for b in range(DRAIN, NB):
                ev_attnT(b - 1)
                if b + 2 < NB:
                    exps(b + 2, 0)
                    exps(b + 2, 1)
                if b == DRAIN:
                    ev_x2T(0)
                    norm2(0, range(6, 2 * CB))
                elif b == DRAIN + 1:
                    std_x2(2, 3)
                elif b == DRAIN + 2:
                    ev_x2T(1)
                    norm2(1, range(2 * CB, 3 * CB))
            ev_attnT(NB - 1)
            ev_x2T(2)
            std_x2(NC - 1, NC)
            norm2(2, range(LAST, NB, 2))
            ev_x2T(NC - 1)

            pad_regions(act, mybir.EngineType.Activation, NE // 2, NE)

            def ev_bT(k):
                act.wait_ge(bT_mm, k + 1)
                if k >= 2:
                    act.wait_ge(h_mm, 2 * (k - 1))
                act.activation(bT[:, k % 2, :], bankA[k % 2][:, 0:128], ACT.Copy).then_inc(bT_ev, 1)

            def blocks(k0, k1):
                ev_bT(k0)
                for k in range(k0, k1):
                    if k + 1 < k1:
                        ev_bT(k + 1)
                    act.wait_ge(h_mm, 2 * k + 1)
                    act.wait_ge(w_in[k % WBUF], 16 * (k // WBUF + 1))
                    if k >= 2:
                        act.wait_ge(y_mm, k - 1)
                    for c in range(2):
                        act.activation(hT[:, k % 2, c, :], bankC_[2 * (k % 2)][:, c * 128:c * 128 + 128], ACT.Relu,
                                       bias=wblk[:, k % WBUF, W_B1 + c:W_B1 + c + 1]).then_inc(h_act, 1)

            blocks(0, SURE)
            act.wait_ge(block_rows, 2)
            with more_blocks(act, mybir.EngineType.Activation):
                blocks(SURE, NBLK)

        @block.vector
        def _(dve):
            def scale1(c):
                s = slice(c * CB, (c + 1) * CB)
                dve.wait_ge(std1, c + 1)
                dve.reciprocal(rstd[:, s], std[:, s]).then_inc(rst1, 1)
                dve.wait_ge(rst1, c + 1)
                dve.scalar_tensor_tensor(nmr[:, s], mv[:, s, 0], -1.0, rstd[:, s], ALU.mult, ALU.mult).then_inc(nmr1, 1)

            dve.memset(attn[:].bitcast(U32), 0).then_inc(attn_zero, 1)
            dve.memset(eps_col[:], EPS).then_inc(eps_set, 1)
            for g in range(NG - 1):
                dve.memset(q_st[:, g, :, TOKS[0]].bitcast(U32), 0).then_inc(q_zero[0], 1)

            def stats_x(c):
                dve.wait_ge(ld_x[c], 16)
                for b in range(c * CB, (c + 1) * CB):
                    dve.bn_stats(stats[:, b, :], x_sb[:, b, :]).then_inc(bn1, 1)
                for b in range(c * CB, (c + 1) * CB):
                    dve.wait_ge(bn1, b + 1)
                    dve.bn_aggr(mv[:, b, :], stats[:, b, :]).then_inc(agg1, 1)

            def k_lo_part(c):
                dve.wait_ge(k_hi, c + 1)
                dve.scalar_tensor_tensor(k_part[:, c % 2, 1, :], kbank, cols_sb[:, 1:2], k_part[:, c % 2, 0, :],
                                         ALU.add, ALU.subtract).then_inc(k_lo, 1)

            def v_lo_part(c):
                dve.wait_ge(v_hi, c + 1)
                if c == 0:
                    dve.wait_ge(v_init, 2)
                dve.tensor_tensor(v_sb[:, c * CB:(c + 1) * CB, :, DH + 1:VC - 1],
                                  vbank.rearrange("p (b h d) -> p b h d", b=CB, h=NH),
                                  v_sb[:, c * CB:(c + 1) * CB, :, 0:DH], ALU.subtract).then_inc(v_lo, 1)

            def q_lo_part(c):
                dve.wait_ge(q_hi, c + 1)
                dve.scalar_tensor_tensor(q_part[:, c % 2, 1, :], qbank, cols_sb[:, 0:1], q_part[:, c % 2, 0, :],
                                         ALU.add, ALU.subtract).then_inc(q_lo, 1)

            stats_x(0)
            scale1(0)
            dve.wait_ge(nmr1, 1)
            for b in range(CB):
                dve.tensor_scalar(xn[:, 0, b, :], x_sb[:, b, :], rstd[:, b:b + 1], nmr[:, b:b + 1],
                                  ALU.mult, ALU.add).then_inc(xn_dve, 1)
            stats_x(1)
            dve.wait_ge(ld_const, 16)
            k_lo_part(0)
            scale1(1)
            stats_x(2)
            q_lo_part(0)
            scale1(2)
            stats_x(3)
            v_lo_part(0)
            k_lo_part(1)
            scale1(3)
            q_lo_part(1)
            v_lo_part(1)
            dve.tensor_copy(token_row[:, :, 2 * D:ROW].bitcast(I32),
                            cf[:, C_TOK:C_TOK + NB].unsqueeze(2).to_broadcast([128, NB, ROW - 2 * D])).then_inc(ids_done, 1)

            def rowmax(b, g):
                dve.wait_ge(s1_mm, 4 * b + g + 1)
                if b >= 2 and g == 0:
                    dve.wait_ge(m_lo, b - 1)
                dve.tensor_reduce(mx[:, b % 2, 4 * g:4 * g + 4], bankA[g % 2][:].rearrange("p (i s) -> p i s", i=4),
                                  axis=AX.X, op=ALU.max).then_inc(max_done, 1)

            def max_parts(b, n):
                m = mx[:, b % 2, :].rearrange("p (g i) -> p g i", g=NG)
                c = mcol[:, b % 2, :].rearrange("p (g i n) -> p g i n", g=NG, n=2)
                if n == 0:
                    dve.wait_ge(max_done, 4 * b + 4)
                    if b >= 2:
                        dve.wait_ge(mT_mm, b - 1)
                    dve.tensor_scalar(c[:, :, :, 0], m, -1.0, None, ALU.mult).then_inc(m_hi, 1)
                else:
                    dve.wait_ge(m_hi, b + 1)
                    dve.scalar_tensor_tensor(c[:, :, :, 1], m, -1.0, c[:, :, :, 0], ALU.mult, ALU.subtract).then_inc(m_lo, 1)

            def lo_part(b):
                s = slice(lo_heads(b) * T, NH * T)
                dve.wait_ge(exp_done, 2 * b + 2)
                if b >= 2:
                    dve.wait_ge(pv_mm, 4 * (b - 1))
                dve.tensor_tensor(prob_lo[:, b % 2, s], prob[:, b % 2, s], hi_of(prob[:, b % 2, s]),
                                  ALU.subtract).then_inc(lo_dve, 1)

            def sum_parts(b):
                dve.wait_ge(pv_mm, 4 * (b + 1))
                if b >= 1:
                    dve.wait_ge(attn_done, b)
                u = bankU[:, 0:NH * VC].rearrange("p (h n c) -> p h c n", h=NH, n=2)
                dve.tensor_reduce(usum[:], u, axis=AX.X, op=ALU.add).then_inc(usum_done, 1)

            def invert(b):
                dve.wait_ge(usum_done, b + 1)
                dve.reciprocal(rden[:], usum[:, :, DH]).then_inc(rden_done, 1)

            def normalise(b):
                dve.wait_ge(rden_done, b + 1)
                if b >= 2:
                    dve.wait_ge(attnT_mm, b - 1)
                dve.tensor_tensor(attn[:, b % 2, :].rearrange("p (h d) -> p h d", h=NH), usum[:, :, 0:DH],
                                  rden[:].unsqueeze(2).to_broadcast([128, NH, DH]), ALU.mult).then_inc(attn_done, 1)

            def residual(b):
                dve.wait_ge(wo_mm, b + 1)
                dve.wait_ge(xb_done, b // CB + 1)
                dve.scalar_tensor_tensor(token_row[:, b, D:2 * D], bankX[:, 128:256], tg[:, 0:1], x_sb[:, b, :],
                                         ALU.mult, ALU.add).then_inc(x2_done, 1)

            def stats_x2(b):
                dve.wait_ge(x2_done, b + 1)
                dve.bn_stats(stats2[:, b, :], token_row[:, b, D:2 * D]).then_inc(bn2, 1)

            def aggr_x2(b):
                dve.wait_ge(bn2, b + 1)
                dve.bn_aggr(mv2[:, b, :], stats2[:, b, :]).then_inc(agg2, 1)

            def scale_x2(n, c0, c1):
                s = slice(c0 * CB, c1 * CB)
                dve.wait_ge(std2_done, n + 1)
                dve.reciprocal(rstd2[:, s], std2[:, s]).then_inc(rst2, 1)
                dve.wait_ge(rst2, n + 1)
                dve.scalar_tensor_tensor(nmr2[:, s], mv2[:, s, 0], -1.0, rstd2[:, s], ALU.mult, ALU.mult).then_inc(nmr2_done, 1)

            def ev_gate(c):
                dve.wait_ge(gate_mm, c + 1)
                dve.tensor_tensor(logit[:, c * CB:(c + 1) * CB, :],
                                  bankA[1][:, 0:CB * NE].rearrange("p (b e) -> p b e", b=CB),
                                  vec_sb[:, V_GB:V_GB + NE].unsqueeze(1).to_broadcast([128, CB, NE]), ALU.add).then_inc(gate_ev, 1)

            steps = [0]

            def step(ins):
                steps[0] += 1
                ins.then_inc(route, 1)
                dve.wait_ge(route, steps[0])

            def choose(c):
                s = slice(c * CB, (c + 1) * CB)

                def wide(a):
                    return a.unsqueeze(2).to_broadcast([128, CB, NE])
                dve.wait_ge(gate_ev, c + 1)
                step(dve.tensor_reduce(lmax[:, s], logit[:, s], axis=AX.X, op=ALU.max))
                step(dve.tensor_tensor(isbest[:, s], logit[:, s], wide(lmax[:, s]), ALU.is_equal))
                step(dve.tensor_tensor(wgt[:, s], isbest[:, s], cf[:, C_E:C_E + NE].unsqueeze(1).to_broadcast([128, CB, NE]),
                                       ALU.mult))
                step(dve.tensor_reduce(wmax[:, s], wgt[:, s], axis=AX.X, op=ALU.max))
                dve.tensor_tensor(onehot_h[:, s], wgt[:, s], wide(wmax[:, s]), ALU.is_equal).then_inc(onehot_done, 1)

            def place(c):
                s = slice(c * CB, (c + 1) * CB)
                dve.wait_ge(onehot_done, c + 1)
                dve.wait_ge(rank_mm, c + 1)
                dve.tensor_tensor(base[:, s], bankC_[0][:, 0:CB * NE].rearrange("p (b e) -> p b e", b=CB),
                                  cf[:, C_REG:C_REG + NE].unsqueeze(1).to_broadcast([128, CB, NE]), ALU.add).then_inc(base_done, 1)
                dve.wait_ge(base_done, c + 1)
                step(dve.tensor_tensor(picked[:, s], base[:, s], onehot_h[:, s], ALU.mult))
                step(dve.tensor_reduce(slotf[:, s], picked[:, s], axis=AX.X, op=ALU.add))
                dve.tensor_copy(slot[:, s], slotf[:, s]).then_inc(slot_done, 1)

            for i in range(NB):
                out_b = i - OUT_LAG
                if i >= 1:
                    max_parts(i - 1, 0)
                rowmax(i, 0)
                if i >= 1:
                    max_parts(i - 1, 1)
                if 1 <= i < 3:
                    q_lo_part(i + 1)
                if out_b >= 0:
                    sum_parts(out_b)
                if i >= PV_LAG:
                    lo_part(i - PV_LAG)
                rowmax(i, 1)
                if out_b >= 0:
                    invert(out_b)
                if out_b >= 1:
                    residual(out_b - 1)
                rowmax(i, 2)
                if out_b >= 0:
                    normalise(out_b)
                if i < 2:
                    k_lo_part(i + 2)
                if out_b >= 1:
                    stats_x2(out_b - 1)
                if i == NORM2_ROUND + 1:
                    scale_x2(0, 0, 2)
                rowmax(i, 3)
                if i < 2:
                    v_lo_part(i + 2)
                if out_b >= 1:
                    aggr_x2(out_b - 1)

            max_parts(NB - 1, 0)
            sum_parts(DRAIN - 1)
            max_parts(NB - 1, 1)
            invert(DRAIN - 1)
            normalise(DRAIN - 1)
            lo_part(DRAIN)
            for b in range(DRAIN, NB):
                residual(b - 2)
                stats_x2(b - 2)
                sum_parts(b)
                invert(b)
                aggr_x2(b - 2)
                normalise(b)
                if b + 1 < NB:
                    lo_part(b + 1)
                if b == DRAIN + 1:
                    ev_gate(0)
                    choose(0)
                elif b == DRAIN + 2:
                    scale_x2(1, 2, 3)
                    place(0)
            residual(NB - 2)
            stats_x2(NB - 2)
            ev_gate(1)
            aggr_x2(NB - 2)
            choose(1)
            place(1)
            residual(NB - 1)
            stats_x2(NB - 1)
            aggr_x2(NB - 1)

            scale_x2(2, NC - 1, NC)
            dve.wait_ge(nmr2_done, 3)
            for b in range(LAST + 1, NB, 2):
                dve.tensor_scalar(token_row[:, b, 0:D], token_row[:, b, D:2 * D], rstd2[:, b:b + 1], nmr2[:, b:b + 1],
                                  ALU.mult, ALU.add).then_inc(xn2_dve, 1)
            ev_gate(2)
            choose(2)
            place(2)
            ev_gate(NC - 1)
            choose(NC - 1)
            dve.wait_ge(count_mm, 1)
            dve.tensor_tensor(steer[:, NBLK:NBLK + NE], bankU[:, 0:NE], cf[:, C_REG:C_REG + NE], ALU.add).then_inc(pad_rows, 1)
            place(NC - 1)
            dve.wait_ge(fill_done, 2)
            step(dve.tensor_tensor(nbc, bankU[:, 0:NE].unsqueeze(2).to_broadcast([128, NE, NB]),
                                   cf[:, C_J:C_J + NE * NB].rearrange("p (e j) -> p e j", e=NE), ALU.is_gt))
            step(dve.tensor_reduce(nblk[:], nbc, axis=AX.X, op=ALU.add))
            step(dve.tensor_tensor_scan(bend[:], ones8[:], nblk[:], 0.0, ALU.mult, ALU.add))
            step(dve.tensor_tensor(ble, bend[:].unsqueeze(1).to_broadcast([128, NBLK, NE]),
                                   cf[:, C_B:C_B + NBLK * NE].rearrange("p (n e) -> p n e", n=NBLK), ALU.is_le))
            step(dve.tensor_tensor(bgone, ble, nblk[:].unsqueeze(1).to_broadcast([128, NBLK, NE]), ALU.mult))
            step(dve.tensor_reduce(bexpf[:], ble, axis=AX.X, op=ALU.add))
            step(dve.tensor_reduce(bgonef[:], bgone, axis=AX.X, op=ALU.add))
            step(dve.scalar_tensor_tensor(bwithin[:], bgonef[:], -128.0, cf[:, C_B128:C_B128 + NBLK], ALU.mult, ALU.add))
            step(dve.scalar_tensor_tensor(browf[:], bexpf[:], float(REGION), bwithin[:], ALU.mult, ALU.add))
            dve.tensor_scalar(steer[:, 0:NBLK], browf[:], float(SPARE), None, ALU.min).then_inc(block_rows, 1)
            dve.tensor_scalar(steer[:, NBLK + NE:], bexpf[:], float(NE - 1), None, ALU.min).then_inc(block_rows, 1)

            def relu(k):
                dve.wait_ge(h_mm, 2 * k + 2)
                dve.wait_ge(w_in[k % WBUF], 16 * (k // WBUF + 1))
                if k >= 2:
                    dve.wait_ge(y_mm, k - 1)
                for c in range(2, 4):
                    dve.tensor_scalar(hT[:, k % 2, c, :], bankC_[2 * (k % 2) + 1][:, (c - 2) * 128:(c - 1) * 128],
                                      wblk[:, k % WBUF, W_B1 + c:W_B1 + c + 1], 0.0, ALU.add, ALU.max).then_inc(h_dve, 1)

            def finish(k):
                dve.wait_ge(y_mm, k + 1)
                dve.wait_ge(res_done, k + 1)
                if k >= OBUF:
                    dve.wait_ge(out_sent[k % OBUF], 16 * (k // OBUF))
                dve.scalar_tensor_tensor(outb[:, k % OBUF, :], [bankU, bankX][k % 2][:, 0:D], tg[:, 1:2], res[:, k % 2, :],
                                         ALU.mult, ALU.add).then_inc(out_done, 1)

            def blocks(k0, k1):
                for k in range(k0, k1):
                    relu(k)
                    if k > k0:
                        finish(k - 1)
                finish(k1 - 1)

            blocks(0, SURE)
            dve.wait_ge(block_rows, 2)
            with more_blocks(dve, mybir.EngineType.DVE):
                blocks(SURE, NBLK)

        @block.tensor
        def _(pe):
            def keep_busy(n, bank, weights, cols):
                for _ in range(n):
                    pe.matmul(bank[:, 0:cols.shape[-1]], weights, cols, start=True, stop=True)

            pe.wait_ge(attn_zero, 1)
            zeros = attn[:].rearrange("p n d -> p (n d)").bitcast(F16)
            keep_busy(BUSY_AT_START, bankX, zeros[:, 0:128], zeros)
            pe.wait_ge(ld_const, 16)

            def project_k(c):
                pe.wait_ge(ld_ctx[c], 16)
                if c:
                    pe.wait_ge(k_lo, c)
                pe.matmul(kbank, w_sb[:, 1, :], ctx_sb[:, TOKS[c]], start=True, stop=True).then_inc(k_mm, 1)

            def transpose_x(c):
                if c:
                    pe.wait_ge(xn_pool, CB * c)
                    pe.wait_ge(xnT_ev, c)
                else:
                    pe.wait_ge(xn_dve, CB)
                for j in range(CB):
                    ins = pe.transpose(xbank[:, j * T:(j + 1) * T], xn[:, c % 2, j, :], ident)
                ins.then_inc(xnT_mm, 1)

            def project_v(c):
                if c:
                    pe.wait_ge(v_lo, c)
                for j in range(CB):
                    b = c * CB + j
                    ins = pe.matmul(vbank[:, j * D:(j + 1) * D], ctx_sb[:, b * T:(b + 1) * T], w_sb[:, 2, :],
                                    start=True, stop=True)
                ins.then_inc(v_mm, 1)

            def project_q(c):
                pe.wait_ge(xnT_ev, c + 1)
                if c:
                    pe.wait_ge(q_lo, c)
                pe.matmul(qbank, w_sb[:, 0, :], xnT[:, c % 2, :], start=True, stop=True).then_inc(q_mm, 1)

            for c in range(2):
                project_k(c)
                transpose_x(c)
                project_q(c)
                project_v(c)
            pe.wait_ge(fill_done, 3)
            pe.wait_ge(ld_vec, 16)
            pe.matmul(bankX[:, 0:D], cols_sb[:, 2:3].to_broadcast([128, 128]), w_sb[:, 3, :], start=True, stop=False)
            pe.matmul(bankX[:, 0:D], ones_row[:], vec_sb[0:1, V_BO:V_BO + D], start=False, stop=True).then_inc(bias_mm, 1)

            def scores(b, g):
                if b or g >= 2:
                    pe.wait_ge(max_done, 4 * b + g - 1)
                if g == 0:
                    pe.wait_ge(k_ready[b // CB], 16)
                    pe.wait_ge(q_ready[b // CB], 64)
                for i in range(4):
                    ins = pe.matmul(bankA[g % 2][:, i * T:(i + 1) * T], q_st[:, g, i, b * T:(b + 1) * T],
                                    k_st[:, g, b * T:(b + 1) * T], start=True, stop=True)
                ins.then_inc(s1_mm, 1)

            def shifted(b, g):
                if g == 0:
                    pe.wait_ge(m_ready[b % 4], 64 * (b // 4 + 1))
                if b >= 1 and g % 2 == 0:
                    pe.wait_ge(exp_done, 2 * b - 1 + g // 2)
                if b == 0 and g == 0:
                    pe.wait_ge(k_lo, NC)
                    pe.wait_ge(v_lo, NC)
                    pe.wait_ge(v_hi, NC)
                    pe.wait_ge(q_lo, NC)
                pe.matmul(bankC_[g].rearrange("p (i t) -> p i t", i=4), k_st[:, g, b * T:(b + 1) * T],
                          q_st[:, g, :, b * T:(b + 1) * T], start=True, stop=True).then_inc(s2_mm, 1)

            def times_v(b, g):
                if g == 0:
                    pe.wait_ge(usum_done, b) if b else pe.wait_ge(xnT_ev, NC)
                if g % 2 == 0:
                    pe.wait_ge(exp_done, 2 * b + 1 + g // 2)
                if g == 0 or (g == 2 and b < DRAIN):
                    pe.wait_ge(lo_pool, lo_count(b, g // 2))
                if g == (3 if b < DRAIN else 2):
                    pe.wait_ge(lo_dve, b + 1)
                for h in range(4 * g, 4 * g + 4):
                    u = bankU[:, h * VC:(h + 1) * VC]
                    s = slice(h * T, (h + 1) * T)
                    pe.matmul(u, hi_of(prob[:, b % 2, s]), v_sb[:, b, h, :], start=True, stop=False)
                    ins = pe.matmul(u, prob_lo[:, b % 2, s], v_sb[:, b, h, :], start=False, stop=True)
                ins.then_inc(pv_mm, 1)


            def max_T(b):
                i = b + 1
                pe.wait_ge(m_lo, b + 1)
                pe.wait_ge(ld_half, 16)
                if b == NB - 1:
                    pe.wait_ge(max_done, 4 * NB)
                elif i > OUT_LAG:
                    pe.wait_ge(x2_done, i - OUT_LAG)
                elif b:
                    pe.wait_ge(mT_ev, b)
                else:
                    pe.wait_ge(gbias_done, 1)
                for g in range(NG):
                    ins = pe.transpose(max_bank(b)[0:8, g * T // 2:(g + 1) * T // 2].bitcast(F16),
                                       mcol[:, b % 2, 8 * g:8 * g + 8], ident_h)
                ins.then_inc(mT_mm, 1)

            def attn_T(b):
                i = b + OUT_LAG
                pe.wait_ge(attn_done, b + 1)
                pe.wait_ge(mT_ev, min(NB - 1, i))
                if b:
                    pe.wait_ge(x2_done, b)
                pe.transpose(bankX[:, 0:T], attn[:, b % 2, :], ident).then_inc(attnT_mm, 1)

            def times_wo(b):
                pe.wait_ge(attnT_ev, b + 1)
                pe.matmul(bankX[:, 128:256], attnT[:, b % 2, :], w_sb[:, 3, :], start=True, stop=True).then_inc(wo_mm, 1)


            def x2_T(c):
                if c:
                    pe.wait_ge(x2T_ev, c)
                else:
                    pe.wait_ge(mT_ev, NB)
                for j in range(CB):
                    b = c * CB + j
                    pe.wait_ge(xn2_act, of_act(b))
                    if of_dve(b):
                        pe.wait_ge(xn2_dve, of_dve(b))
                    ins = pe.transpose(bankA[0][:, j * T:(j + 1) * T], token_row[:, b, 0:D], ident)
                ins.then_inc(x2T_mm, 1)

            def gate(c):
                if c:
                    pe.wait_ge(gate_ev, c)
                else:
                    pe.wait_ge(max_done, 4 * NB)
                pe.wait_ge(x2T_ev, c + 1)
                for j in range(CB):
                    ins = pe.matmul(bankA[1][:, j * NE:(j + 1) * NE], x2T[:, j * T:(j + 1) * T], gate_sb, start=True, stop=True)
                ins.then_inc(gate_mm, 1)

            def rank(c):
                pe.wait_ge(onehot_done, c + 1)
                if c:
                    pe.wait_ge(base_done, c)
                else:
                    pe.wait_ge(exp_done, 2 * NB)
                bank = bankC_[0]
                own = onehot_h[:, c * CB:(c + 1) * CB, :].rearrange("p b e -> p (b e)")
                pe.matmul(bank[:, 0:CB * NE], before_h, own, start=True, stop=False)
                for j in range(c * CB):
                    pe.matmul(bank[:, 0:CB * NE], ones_h, onehot_h[:, j, :].unsqueeze(1).to_broadcast([128, CB, NE]),
                              start=False, stop=False)
                for j in range(1, CB):
                    ins = pe.matmul(bank[:, j * NE:CB * NE], ones_h, own[:, 0:(CB - j) * NE], start=False, stop=(j == CB - 1))
                ins.then_inc(rank_mm, 1)

            scores(0, 0)
            for i in range(NB):
                s2_b, pv_b, out_b = i - S2_LAG, i - PV_LAG, i - OUT_LAG
                scores(i, 1)
                if s2_b >= 0:
                    shifted(s2_b, 0)
                    shifted(s2_b, 1)
                if i >= 2:
                    scores(i, 2)
                else:
                    project_k(i + 2)
                    scores(i, 2)
                    project_v(i + 2)
                if out_b >= 1:
                    times_wo(out_b - 1)
                if i < 2:
                    transpose_x(i + 2)
                if pv_b >= 0:
                    times_v(pv_b, 0)
                    times_v(pv_b, 1)
                if s2_b >= 0:
                    shifted(s2_b, 2)
                scores(i, 3)
                if i >= 1:
                    max_T(i - 1)
                if pv_b >= 0:
                    times_v(pv_b, 2)
                if s2_b >= 0:
                    shifted(s2_b, 3)
                if pv_b >= 0:
                    times_v(pv_b, 3)
                if i + 1 < NB:
                    scores(i + 1, 0)
                if i < 2:
                    project_q(i + 2)
                if out_b >= 0:
                    attn_T(out_b)

            max_T(NB - 1)
            for g in range(NG):
                shifted(DRAIN + 1, g)
            times_wo(DRAIN - 2)
            for b in range(DRAIN, NB):
                for g in range(NG):
                    times_v(b, g)
                if b == NB - 1:
                    gate(1)
                if b == NB - 2:
                    pe.wait_ge(exp_done, 2 * NB - 1)
                    keep_busy(5, bankC_[1], ident_h, ch[:])
                attn_T(b - 1)
                if b + 2 < NB:
                    for g in range(NG):
                        shifted(b + 2, g)
                else:
                    keep_busy(3, bankC_[1], ident_h, ch[:])
                times_wo(b - 1)
                if b == DRAIN:
                    x2_T(0)
                elif b == DRAIN + 1:
                    gate(0)
                elif b == DRAIN + 2:
                    x2_T(1)
                    rank(0)
            keep_busy(3, bankC_[1], ident_h, ch[:])
            attn_T(NB - 1)
            x2_T(2)
            times_wo(NB - 1)
            rank(1)
            keep_busy(2, bankC_[1], ident_h, ch[:])
            gate(2)
            keep_busy(13, bankC_[1], ident_h, ch[:])
            x2_T(3)
            rank(2)
            gate(3)
            keep_busy(7, bankC_[1], ident_h, ch[:])
            pe.wait_ge(onehot_done, NC)
            pe.wait_ge(usum_done, NB)
            for b in range(NB):
                ins = pe.matmul(bankU[:, 0:NE], ones_h, onehot_h[:, b, :], start=(b == 0), stop=(b == NB - 1))
            ins.then_inc(count_mm, 1)
            rank(NC - 1)

            def block_T(k):
                pe.wait_ge(blk_in[k % NBUF], 16 * (k // NBUF + 1))
                if k >= 2:
                    pe.wait_ge(bT_ev, k - 1)
                else:
                    pe.wait_ge(base_done, NC)
                pe.transpose(bankA[k % 2][:, 0:128], blk[:, k % NBUF, 0:D], ident).then_inc(bT_mm, 1)

            def hidden(k):
                pe.wait_ge(bT_ev, k + 1)
                pe.wait_ge(w_in[k % WBUF], 16 * (k // WBUF + 1))
                if k >= 2:
                    pe.wait_ge(h_act, 2 * (k - 1))
                    pe.wait_ge(h_dve, 2 * (k - 1))
                else:
                    pe.wait_ge(base_done, NC)
                for half in range(2):
                    for c in range(2):
                        ins = pe.matmul(bankC_[2 * (k % 2) + half][:, c * 128:(c + 1) * 128],
                                        wblk[:, k % WBUF, (2 * half + c) * 128:(2 * half + c + 1) * 128], bT[:, k % 2, :],
                                        start=True, stop=True)
                    ins.then_inc(h_mm, 1)

            def down(k):
                pe.wait_ge(h_act, 2 * (k + 1))
                pe.wait_ge(h_dve, 2 * (k + 1))
                if k >= 2:
                    pe.wait_ge(out_done, k - 1)
                for c in range(HC):
                    ins = pe.matmul([bankU, bankX][k % 2][:, 0:D], hT[:, k % 2, c, :],
                                    experts[:, bass.ds(block_expert[k], 1), WCOPY + c * D:WCOPY + (c + 1) * D], start=(c == 0), stop=(c == HC - 1))
                ins.then_inc(y_mm, 1)

            pe.wait_ge(base_done, NC)
            keep_busy(BUSY_BEFORE_ROWS, bankA[0], ident_h, ch[:])
            pe.wait_ge(ld_exp, 32 * NE)
            pe.wait_ge(block_rows, 2)
            block_expert = {}

            def load_experts(k, last):
                n = min(4, last - k)
                if n > 0:
                    block_expert.update(zip(range(k, k + n), nc.values_load_multi_w_load_instructions(
                        steer[0:1, NBLK + NE + k:NBLK + NE + k + n], engines=(mybir.EngineType.PE,),
                        min_val=0, max_val=NE - 1)[1]))
            load_experts(0, SURE)
            keep_busy(BUSY_BEFORE_BLOCKS, bankA[0], ident_h, ch[:])

            def blocks(k0, k1):
                block_T(k0)
                for k in range(k0, k1):
                    if k + 1 < k1:
                        block_T(k + 1)
                    hidden(k)
                    if k % 4 == 0:
                        load_experts(k + 4, k1)
                    if k > k0:
                        down(k - 1)
                down(k1 - 1)

            blocks(0, SURE)
            with more_blocks(pe, mybir.EngineType.PE):
                load_experts(SURE, NBLK)
                blocks(SURE, NBLK)


def kernel(x, ctx_1024, g_xattn, g_ffn, L0_xattn_wq_w, L0_xattn_wq_b, L0_xattn_wk_w, L0_xattn_wk_b, L0_xattn_wv_w,
           L0_xattn_wv_b, L0_xattn_wo_w, L0_xattn_wo_b, L0_ffn_gate_w, L0_ffn_gate_b, L0_ffn_w1, L0_ffn_b1, L0_ffn_w2,
           L0_ffn_b2):
    import numpy as np
    import concourse.bacc as bacc
    from concourse.bass_utils import run_bass_kernel_spmd

    a = {n: np.asarray(v) for n, v in dict(
        x=x, ctx=ctx_1024, gx=g_xattn, gf=g_ffn, wq=L0_xattn_wq_w, wk=L0_xattn_wk_w, wv=L0_xattn_wv_w, wo=L0_xattn_wo_w,
        bq=L0_xattn_wq_b, bk=L0_xattn_wk_b, bv=L0_xattn_wv_b, bo=L0_xattn_wo_b, gw=L0_ffn_gate_w, gb=L0_ffn_gate_b,
        w1=L0_ffn_w1, b1=L0_ffn_b1, w2=L0_ffn_w2, b2=L0_ffn_b2).items()}
    p = np.arange(128)
    constf = np.zeros((128, NCONST), np.float32)
    constf[:, C_ID:C_ID + 128] = np.eye(128)
    constf[:, C_W:C_GATE] = np.concatenate([a[n].T for n in ("wq", "wk", "wv", "wo")], 1)
    constf[:, C_GATE:C_COL] = a["gw"].T
    constf[:, C_COL] = a["bq"]
    constf[:, C_COL + 1] = a["bk"]
    constf[:, C_COL + 2] = a["bv"]
    constf[:, C_J:C_J + NE * NB] = np.tile(128.0 * np.arange(NB), NE)
    constf[:, C_E:C_E + NE] = NE - np.arange(NE)
    constf[:, C_B:C_B + NBLK * NE] = np.repeat(np.arange(NBLK), NE)
    constf[:, C_B128:C_B128 + NBLK] = 128 * np.arange(NBLK)
    constf[:, C_REG:C_REG + NE] = REGION * np.arange(NE)
    constf[:, C_TOK:C_TOK + NB] = 128 * np.arange(NB)[None, :] + p[:, None]
    consth = np.concatenate([np.eye(128), p[:, None] < p[None, :], np.ones((128, 128))], 1).astype(np.float16)
    ins = {
        "x": a["x"],
        "ctxT": a["ctx"].transpose(2, 0, 1).reshape(D, NTOK),
        "vecs": np.concatenate([a[n] for n in ("bo", "gb", "gx", "gf")]),
        "wexp": np.concatenate([
            a["w1"].transpose(0, 2, 1),
            a["b1"].reshape(NE, HC, 128).transpose(0, 2, 1),
            a["w2"].transpose(0, 2, 1).reshape(NE, HC, 128, D).transpose(0, 2, 1, 3).reshape(NE, 128, HC * D)], 2),
        "b2r": a["b2"],
        "constf": constf,
        "consth": consth,
        "onesh": np.ones((NG, 4, DH, NTOK), np.float16),
    }
    ins = {n: np.ascontiguousarray(v) for n, v in ins.items()}
    nc = bacc.Bacc("TRN2", target_bir_lowering=False, num_devices=1)
    aps = {n: nc.dram_tensor("in_" + n, v.shape, mybir.dt.from_np(v.dtype), kind="ExternalInput").ap() for n, v in ins.items()}
    out = nc.dram_tensor("out", (NTOK, D), F32, kind="ExternalOutput").ap()
    program(nc, **aps, out=out)
    r = run_bass_kernel_spmd(nc, [{"in_" + n: v for n, v in ins.items()}], core_ids=[0])
    return r.results[0]["out"].reshape(NB, T, D)
```
